# Optimizing a Trainium2 kernel written in Bass

```python
import numpy as np
import jax
import jax.numpy as jnp

def _softmax(x, axis=-1):
    return jax.nn.softmax(x, axis=axis)

def _gelu(x):
    return jax.nn.gelu(x, approximate=True)

def _silu(x):
    return jax.nn.silu(x)

def _sigmoid(x):
    return jax.nn.sigmoid(x)

def _layernorm(x, axis=-1, eps=1e-05):
    m = jnp.mean(x, axis=axis, keepdims=True)
    v = jnp.var(x, axis=axis, keepdims=True)
    return (x - m) / jnp.sqrt(v + eps)

def _scatter_add(tgt, idx, src, axis=0):
    return tgt.at[idx].add(src)

def _segment_sum(src, seg, n):
    return jax.ops.segment_sum(src, seg, n)
kernel_name = 'mk_xattn_ffn_d1_seqx_r8_fe9202'

def setup_inputs(seed: int=0):
    np.random.seed(seed)
    _w = jnp.asarray

    def _rec_inputs():
        import jax
        import jax.numpy as jnp
        _rk = jax.random.key(seed)
        x = -9.806e-05 + 1 * jax.random.normal(jax.random.fold_in(_rk, 1), (32, 128, 128), jnp.float32)
        _lenS = 128 - jax.random.randint(jax.random.fold_in(_rk, 7), (32,), 0, max(1, 128 // 4) + 1, jnp.int32)
        _lenS2 = 128 - jax.random.randint(jax.random.fold_in(_rk, 8), (32,), 0, max(1, 128 // 4) + 1, jnp.int32)
        _ctx_1024P = jax.random.normal(jax.random.fold_in(_rk, 11), (32, 16, 128), jnp.float32)
        _ctx_1024c = jax.random.dirichlet(jax.random.fold_in(_rk, 511), 0.3 * jnp.ones((16,), jnp.float32), (32, 128))
        _ctx_1024t = jnp.einsum('bsk,bkd->bsd', _ctx_1024c, _ctx_1024P)
        _ctx_1024t = _ctx_1024t * jax.lax.rsqrt(jnp.mean(jnp.square(_ctx_1024t)) + 1e-12) * 0.953939
        ctx_1024 = -1.52775e-05 + 0.999936 * (_ctx_1024t + 0.3 * jax.random.normal(jax.random.fold_in(_rk, 611), (32, 128, 128), jnp.float32))
        return (x, ctx_1024)
    x, ctx_1024 = _rec_inputs()

    def _L0_xattn_setup():
        import jax, jax.numpy as jnp
        import numpy as np
        D = 128
        NUM_ITERS = 3
        EPS = 1e-06
        SCALE = D ** (-0.5)

        def rmsnorm(x, w, eps=EPS):
            return x * jax.lax.rsqrt(jnp.mean(x * x, axis=-1, keepdims=True) + eps) * w

        def gru_cell(x, h, wih, whh, bih, bhh):
            gx = x @ wih.T + bih
            gh = h @ whh.T + bhh
            xr, xz, xn = jnp.split(gx, 3, axis=-1)
            hr, hz, hn = jnp.split(gh, 3, axis=-1)
            r = jax.nn.sigmoid(xr + hr)
            z = jax.nn.sigmoid(xz + hz)
            n = jnp.tanh(xn + r * hn)
            return (1.0 - z) * n + z * h
        key = jax.random.key(seed)
        ks = jax.random.split(key, 8)
        B, K, M, d = (8, 64, 512, D)
        w_std = d ** (-0.5)
        return {'slots': jax.random.normal(ks[0], (B, K, d), jnp.float32), 'P': jax.random.normal(ks[1], (B, M, d), jnp.float32), 'Wq': jax.random.normal(ks[2], (d, d), jnp.float32) * w_std, 'Wk': jax.random.normal(ks[3], (d, d), jnp.float32) * w_std, 'Wv': jax.random.normal(ks[4], (d, d), jnp.float32) * w_std, 'gru_wih': jax.random.normal(ks[5], (3 * d, d), jnp.float32) * w_std, 'gru_whh': jax.random.normal(ks[6], (3 * d, d), jnp.float32) * w_std, 'gru_bih': jnp.zeros((3 * d,), jnp.float32), 'gru_bhh': jnp.zeros((3 * d,), jnp.float32), 'slot_norm_w': jnp.ones((d,), jnp.float32), 'input_norm_w': jnp.ones((d,), jnp.float32)}
    _L0_xattn_all = _L0_xattn_setup()
    _L0_xattn_in = {k: v for k, v in _L0_xattn_all.items() if k in ('Wq', 'Wk', 'Wv', 'gru_wih', 'gru_whh', 'gru_bih', 'gru_bhh', 'slot_norm_w', 'input_norm_w')}
    del _L0_xattn_all

    def _L0_ffn_setup():
        import jax, jax.numpy as jnp
        import numpy as np
        B, S, D, F, E, K = (2, 256, 128, 512, 8, 2)
        key = jax.random.key(seed)
        ks = jax.random.split(key, 5)
        x = jax.random.normal(ks[0], (B, S, D), dtype=jnp.float32)
        Wg = jax.random.normal(ks[1], (D, E), dtype=jnp.float32) * 0.02
        W1 = jax.random.normal(ks[2], (E, D, F), dtype=jnp.float32) * 0.02
        b1 = jnp.zeros((E, F), dtype=jnp.float32)
        W2 = jax.random.normal(ks[3], (E, F, D), dtype=jnp.float32) * 0.02
        b2 = jnp.zeros((E, D), dtype=jnp.float32)
        return {'x': x, 'Wg': Wg, 'W1': W1, 'b1': b1, 'W2': W2, 'b2': b2}
    _L0_ffn_all = _L0_ffn_setup()
    _L0_ffn_in = {k: v for k, v in _L0_ffn_all.items() if k in ('Wg', 'W1', 'b1', 'W2', 'b2')}
    del _L0_ffn_all
    return {'x': x, 'ctx_1024': ctx_1024, 'L0_xattn_Wq': _L0_xattn_in['Wq'], 'L0_xattn_Wk': _L0_xattn_in['Wk'], 'L0_xattn_Wv': _L0_xattn_in['Wv'], 'L0_xattn_gru_wih': _L0_xattn_in['gru_wih'], 'L0_xattn_gru_whh': _L0_xattn_in['gru_whh'], 'L0_xattn_gru_bih': _L0_xattn_in['gru_bih'], 'L0_xattn_gru_bhh': _L0_xattn_in['gru_bhh'], 'L0_xattn_slot_norm_w': _L0_xattn_in['slot_norm_w'], 'L0_xattn_input_norm_w': _L0_xattn_in['input_norm_w'], 'L0_ffn_Wg': _L0_ffn_in['Wg'], 'L0_ffn_W1': _L0_ffn_in['W1'], 'L0_ffn_b1': _L0_ffn_in['b1'], 'L0_ffn_W2': _L0_ffn_in['W2'], 'L0_ffn_b2': _L0_ffn_in['b2']}

def reference(x, ctx_1024, L0_xattn_Wq, L0_xattn_Wk, L0_xattn_Wv, L0_xattn_gru_wih, L0_xattn_gru_whh, L0_xattn_gru_bih, L0_xattn_gru_bhh, L0_xattn_slot_norm_w, L0_xattn_input_norm_w, L0_ffn_Wg, L0_ffn_W1, L0_ffn_b1, L0_ffn_W2, L0_ffn_b2):
    import jax
    import jax.numpy as jnp

    def _L0_xattn_ref(slots, P, Wq, Wk, Wv, gru_wih, gru_whh, gru_bih, gru_bhh, slot_norm_w, input_norm_w):
        import jax, jax.numpy as jnp
        import numpy as np
        D = 128
        NUM_ITERS = 3
        EPS = 1e-06
        SCALE = D ** (-0.5)

        def rmsnorm(x, w, eps=EPS):
            return x * jax.lax.rsqrt(jnp.mean(x * x, axis=-1, keepdims=True) + eps) * w

        def gru_cell(x, h, wih, whh, bih, bhh):
            gx = x @ wih.T + bih
            gh = h @ whh.T + bhh
            xr, xz, xn = jnp.split(gx, 3, axis=-1)
            hr, hz, hn = jnp.split(gh, 3, axis=-1)
            r = jax.nn.sigmoid(xr + hr)
            z = jax.nn.sigmoid(xz + hz)
            n = jnp.tanh(xn + r * hn)
            return (1.0 - z) * n + z * h
        Pn = rmsnorm(P, input_norm_w)
        k_proj = Pn @ Wk.T
        v_proj = Pn @ Wv.T
        for _ in range(NUM_ITERS):
            sn = rmsnorm(slots, slot_norm_w)
            q_proj = sn @ Wq.T
            scores = jnp.einsum('bkd,bmd->bkm', q_proj, k_proj) * SCALE
            attn = jax.nn.softmax(scores, axis=-2)
            attn = attn / (jnp.sum(attn, axis=-1, keepdims=True) + EPS)
            updates = jnp.einsum('bkm,bmd->bkd', attn, v_proj)
            slots = gru_cell(updates, slots, gru_wih, gru_whh, gru_bih, gru_bhh)
        return slots

    def _L0_ffn_ref(x, Wg, W1, b1, W2, b2):
        import jax, jax.numpy as jnp
        import numpy as np
        B, S, D, F, E, K = (2, 256, 128, 512, 8, 2)
        b, s, d = x.shape
        e = Wg.shape[1]
        T = b * s
        C = 2 * K * T // e
        xt = x.reshape(T, d)
        logits = xt.astype(jnp.float32) @ Wg.astype(jnp.float32)
        gates = jax.nn.softmax(logits, axis=-1)
        idx1 = jnp.argmax(gates, axis=-1)
        mask1 = jax.nn.one_hot(idx1, e, dtype=gates.dtype)
        gate1 = jnp.sum(gates * mask1, axis=-1)
        logits2 = jnp.where(mask1 > 0, -jnp.inf, logits)
        idx2 = jnp.argmax(logits2, axis=-1)
        mask2 = jax.nn.one_hot(idx2, e, dtype=gates.dtype)
        gate2 = jnp.sum(gates * mask2, axis=-1)
        denom = gate1 + gate2 + 1e-09
        w1 = gate1 / denom
        w2 = gate2 / denom
        p1 = jnp.cumsum(mask1, axis=0) - mask1
        pos1 = jnp.sum(p1 * mask1, axis=-1).astype(jnp.int32)
        off = jnp.sum(mask1, axis=0)
        p2 = jnp.cumsum(mask2, axis=0) - mask2 + off[None, :]
        pos2 = jnp.sum(p2 * mask2, axis=-1).astype(jnp.int32)
        keep1 = (pos1 < C).astype(xt.dtype)
        keep2 = (pos2 < C).astype(xt.dtype)
        pos1 = jnp.clip(pos1, 0, C - 1)
        pos2 = jnp.clip(pos2, 0, C - 1)
        xe = jnp.zeros((e, C, d), dtype=xt.dtype)
        xe = xe.at[idx1, pos1].add(xt * keep1[:, None])
        xe = xe.at[idx2, pos2].add(xt * keep2[:, None])
        h = jax.nn.gelu(jnp.einsum('ecd,edf->ecf', xe, W1) + b1[:, None, :], approximate=False)
        ye = jnp.einsum('ecf,efd->ecd', h, W2) + b2[:, None, :]
        out = ye[idx1, pos1] * (w1 * keep1)[:, None] + ye[idx2, pos2] * (w2 * keep2)[:, None]
        return out.reshape(b, s, d)
    x = x + _L0_xattn_ref(_layernorm(x, axis=-1), ctx_1024, L0_xattn_Wq, L0_xattn_Wk, L0_xattn_Wv, L0_xattn_gru_wih, L0_xattn_gru_whh, L0_xattn_gru_bih, L0_xattn_gru_bhh, L0_xattn_slot_norm_w, L0_xattn_input_norm_w)
    x = x + _L0_ffn_ref(_layernorm(x, axis=-1), L0_ffn_Wg, L0_ffn_W1, L0_ffn_b1, L0_ffn_W2, L0_ffn_b2)
    return x

_drawn_inputs = setup_inputs


def setup_inputs(seed=0):
    import zlib

    import numpy as np

    out = dict(_drawn_inputs(seed))
    spreads = {'L0_xattn_gru_bih': (0.0, 0.1),
     'L0_xattn_gru_bhh': (0.0, 0.1),
     'L0_xattn_slot_norm_w': (1.0, 0.6),
     'L0_xattn_input_norm_w': (1.0, 0.2),
     'L0_ffn_b1': (0.0, 0.596),
     'L0_ffn_b2': (0.0, 0.1)}
    factors = {}
    for name, (base, spread) in spreads.items():
        noise = np.random.default_rng([zlib.crc32(name.encode()), seed]).standard_normal(out[name].shape)
        drawn = base * np.exp(spread * noise) if base else spread * noise
        out[name] = jnp.asarray(drawn.astype(out[name].dtype))
    for name, factor in factors.items():
        out[name] = (out[name] * factor).astype(out[name].dtype)
    return out
```

```python
from contextlib import ExitStack

import concourse.bass as bass
from concourse import mybir

F32 = mybir.dt.float32
BF16 = mybir.dt.bfloat16
U32 = mybir.dt.uint32
I32 = mybir.dt.int32
ALU = mybir.AluOpType
ACT = mybir.ActivationFunctionType
AX = mybir.AxisListType

P = 128


def xattn_moe_kernel(nc, x, ctx, proj, gru, columns, Wg, W1, b1, W2, b2, out):
    B, S, D = x.shape
    E, _, F = W1.shape
    TOP = 2
    T = B * S
    CAP = 2 * TOP * T // E
    NTOK = T // P
    GB = 4
    NG = B // GB
    LANES = 4
    ROUNDS = NG // LANES
    ITERS = 3
    GW = GB * S
    FC = F // P
    TILES = TOP * T // P + E - 1
    NJ = TILES + TILES % 2
    SCALE = float(D) ** -0.5
    QS = CAP // P
    INVALID = 16384.0

    ln_dram = nc.dram_tensor("ln_rows", [T, D], F32, kind="Internal").ap()
    y_dram = nc.dram_tensor("expert_rows", [TOP * T, D], F32, kind="Internal").ap()
    bias_dram = nc.dram_tensor("bias_parts", [3, E * D], BF16, kind="Internal").ap()

    x_g = x.rearrange("(g b) s d -> g s b d", b=GB)
    ctx_g = ctx.rearrange("(g b) s d -> g s b d", b=GB)
    ln_g = ln_dram.rearrange("(g b s) d -> g s b d", b=GB, s=S)

    with ExitStack() as stack:
        def sb(name, shape, dt=F32):
            return stack.enter_context(nc.sbuf_tensor(name, shape, dt))

        def psum(name):
            return stack.enter_context(nc.psum_tensor(name, [P, 512], F32))

        def sem(name):
            return stack.enter_context(nc.semaphore(name))

        def lane_sems(name):
            return [sem(f"{name}{l}") for l in range(LANES)]

        ident = sb("ident", [P, P])
        ones_col = sb("ones_col", [P, 1])
        ones_bf = sb("ones_bf", [P, P], BF16)
        before = sb("before", [P, P], BF16)
        zeros = sb("zeros", [P, 2048])
        neg_half = sb("neg_half", [P, GB])
        proj_in = sb("proj_in", [P, 3, D])
        gru_in = sb("gru_in", [P, 2, 3, D])
        col_in = sb("col_in", [P, 8])
        wkq = sb("wkq", [P, D])
        wvT = sb("wvT", [P, D])
        wihT = gru_in[:, 0]
        whhT = gru_in[:, 1]
        bias_rz = sb("bias_rz", [P, 2])
        bias_hn = sb("bias_hn", [P, 1])
        slot_scale = sb("slot_scale", [P, 1])
        wg_sb = sb("wg_sb", [P, E])
        w1_sb = sb("w1_sb", [P, E, F + FC])
        w2_sb = sb("w2_sb", [P, E, FC, D])
        w1_now = [sb(f"w1_now{b}", [P, F + FC]) for b in range(2)]
        b_in = sb("b_in", [P, E * D // P])
        b_parts = sb("b_parts", [P, 3, E * D // P], BF16)
        b_rest = sb("b_rest", [P, 2, E * D // P])
        b_rows = sb("b_rows", [P, E * D], BF16)
        w1_flat = w1_sb[:, :, :].rearrange("p e f -> p (e f)")
        w2_flat = w2_sb[:, :, :, :].rearrange("p e c d -> p (e c d)")

        x_in = [sb(f"x_in{l}", [P, GB, D]) for l in range(LANES)]
        c_in = [sb(f"c_in{l}", [P, GB, D]) for l in range(LANES)]
        hT = [sb(f"hT{l}", [P, GB, S]) for l in range(LANES)]
        work = [sb(f"work{l}", [P, GB, P]) for l in range(LANES)]
        prob = [sb(f"prob{l}", [P, GB, S]) for l in range(LANES)]
        uT = [sb(f"uT{l}", [P, GB, S]) for l in range(LANES)]
        tr = [sb(f"tr{l}", [P, GB, S]) for l in range(LANES)]
        tz = [sb(f"tz{l}", [P, GB, S]) for l in range(LANES)]
        hn = [sb(f"hn{l}", [P, GB, S]) for l in range(LANES)]
        kq = [sb(f"kq{l}", [P, GB, P]) for l in range(LANES)]
        v = [sb(f"v{l}", [P, GB, D]) for l in range(LANES)]
        rms = [sb(f"rms{l}", [P, GB]) for l in range(LANES)]
        peak = [sb(f"peak{l}", [P, GB]) for l in range(LANES)]
        zsum = [sb(f"zsum{l}", [P, GB]) for l in range(LANES)]
        zinv = [sb(f"zinv{l}", [P, GB]) for l in range(LANES)]
        asum = [sb(f"asum{l}", [P, GB]) for l in range(LANES)]
        ainv = [sb(f"ainv{l}", [P, GB]) for l in range(LANES)]
        stats = [sb(f"stats{l}", [P, GB, 6]) for l in range(LANES)]
        moments = [sb(f"moments{l}", [P, GB, 2]) for l in range(LANES)]
        rstd = [sb(f"rstd{l}", [P, GB]) for l in range(LANES)]
        csum = [sb(f"csum{l}", [P, GB]) for l in range(LANES)]
        crms = [sb(f"crms{l}", [P, GB]) for l in range(LANES)]

        x2 = sb("x2", [P, NTOK, D])
        logits = sb("logits", [P, NTOK, E])
        top8 = sb("top8", [P, NTOK, E])
        top8_at = sb("top8_at", [P, NTOK, E], U32)

        NP = TOP * NTOK
        iota_i = sb("iota_i", [P, P], I32)
        iota_f = sb("iota_f", [P, P])
        row_i = sb("row_i", [P, 1], I32)
        row_f = sb("row_f", [P, 1])
        steps128 = sb("steps128", [P, QS])
        restart = sb("restart", [P, E, NTOK])
        at = sb("at", [P, TOP, NTOK])
        mask = sb("mask", [P, TOP, E, NTOK], BF16)
        upto = sb("upto", [P, TOP, E, NTOK])
        place = sb("place", [P, TOP, E, NTOK])
        pos = sb("pos", [P, TOP, NTOK])
        keep = sb("keep", [P, TOP, NTOK])
        filled = sb("filled", [P, E])
        compare = sb("compare", [P, NP, QS])
        tiles_of = sb("tiles_of", [P, E])
        tile_end = sb("tile_end", [P, E])
        tile_base = sb("tile_base", [P, E])
        base_of = sb("base_of", [P, TOP, NTOK])
        depth = sb("depth", [P, TOP, NTOK])
        in_tile = sb("in_tile", [P, NP])
        which = sb("which", [P, NP])
        hot_row = [sb(f"hot_row{b}", [P, 8, P], BF16) for b in range(2)]
        hot_tile = [sb(f"hot_tile{b}", [P, 8, NJ], BF16) for b in range(2)]
        hot_value = [sb(f"hot_value{b}", [P, 8, 2 * NJ], BF16) for b in range(2)]
        zero_bf = sb("zero_bf", [P, 2 * NJ], BF16)
        rows_f = sb("rows_f", [P, NJ])
        rows_g = sb("rows_g", [P, NJ])
        rows_e = sb("rows_e", [P, NJ])
        to_rows = sb("to_rows", [P, NJ], U32)
        from_rows = sb("from_rows", [P, NJ], U32)
        ended = sb("ended", [1, NJ, E])
        tile_expert_f = sb("tile_expert_f", [1, NJ])
        tile_expert = sb("tile_expert", [1, NJ], I32)
        exps = sb("exps", [P, NTOK, E])
        exp2 = sb("exp2", [P, NTOK])
        gate = [sb(f"gate{c}", [P, NTOK]) for c in range(TOP)]
        gsum = sb("gsum", [P, NTOK])
        denom = sb("denom", [P, NTOK])

        RB = 4
        from_col = [sb(f"from_col{b}", [P, 1], U32) for b in range(RB)]
        to_col = [sb(f"to_col{b}", [P, 1], U32) for b in range(RB)]
        rows = [sb(f"rows{b}", [P, D]) for b in range(RB)]
        results = [sb(f"results{b}", [P, D]) for b in range(RB)]
        rowsT = [sb(f"rowsT{b}", [P, P]) for b in range(2)]
        hiddenT = tz[0:2]

        lane_bank = [psum(f"lane_bank{l}") for l in range(LANES)]
        bank_r, bank_z, bank_hn, bank_xn = (psum(f"bank_{n}") for n in ("r", "z", "hn", "xn"))

        bank_rows = lane_bank[2:4]
        bank_out = lane_bank[0:2]
        bank_hid = [bank_r, bank_z]

        s_ident, s_const = sem("ident_set"), sem("const_set")
        s_wload, s_gload, s_wmoe, s_bload = sem("w_loaded"), sem("gru_w_loaded"), sem("moe_w_loaded"), sem("bias_loaded")
        s_wp, s_we = sem("w_product"), sem("w_evacuated")
        s_bcol = sem("bias_columns")
        s_bpart, s_bstore, s_brow, s_bzero = (sem("bias_part"), sem("bias_parts_stored"),
                                             sem("bias_rows_loaded"), sem("bias_rows_zeroed"))
        s_yzero = sem("y_zeroed")
        s_iota, s_iotaf = sem("iotas"), sem("iotas_float")
        s_route, s_mask, s_count = sem("routing_step"), sem("mask"), sem("counts")
        s_hot, s_hott, s_hotuse, s_table, s_texp = sem("one_hots"), sem("tile_one_hots"), sem("one_hots_used"), sem("table"), sem("tile_expert")
        s_shift, s_gexp = sem("logits_shifted"), sem("gate_exps")
        s_gate = sem("gates_step")
        s_go = sem("rows_may_move")
        s_fcol, s_tcol = sem("from_column"), sem("to_column")
        s_rows = [sem(f"rows_gathered{b}") for b in range(RB)]
        s_back = [sem(f"rows_scattered{b}") for b in range(RB)]
        s_xp, s_xe, s_w1, s_hp, s_ge, s_yp, s_ye = (
            sem(n) for n in ("rows_turned", "rows_turned_copied", "w1_copied", "hidden_product", "hidden_gelu",
                             "out_product", "out_copied"))
        s_yload = [sem(f"y_loaded{l}") for l in range(LANES)]
        s_first, s_both, s_out = sem("first_choice_added"), sem("both_added"), sem("out_stored")
        s_xload, s_cload = lane_sems("x_loaded"), lane_sems("ctx_loaded")
        s_fst_ = lane_sems("ln_stored")
        s_csq, s_cms, s_crms, s_cn, s_cT, s_cTe, s_kq, s_kqe, s_v, s_ve = (
            sem(n) for n in ("ctx_squares", "ctx_mean_square", "ctx_rms", "ctx_normed", "ctx_turned",
                                   "ctx_turned_copied", "kq_product", "kq_copied", "v_product", "v_copied"))
        s_xst, s_xmo, s_xve, s_xrs, s_xn_, s_xT = (
            sem(n) for n in ("x_stats", "x_moments", "x_variance", "x_rstd", "x_normed", "x_turned"))
        s_h0, s_h = sem("h_started"), sem("h_updated")
        s_sq, s_ssq, s_ms, s_rms, s_sc, s_scs, s_scT = (
            sem(n) for n in ("h_squares", "h_square_sum", "h_mean_square", "h_rms", "scores",
                                   "scores_scaled", "scores_turned"))
        s_pk, s_sub, s_exp, s_zs, s_zi, s_at = (
            sem(n) for n in ("peak", "scores_shifted", "exp", "exp_sum", "exp_inverse", "attn"))
        s_as, s_ase, s_ai, s_u, s_un, s_uT, s_uTe = (
            sem(n) for n in ("attn_sum", "attn_sum_copied", "attn_inverse", "update_product",
                                   "update_normed", "update_turned", "update_copied"))
        s_R, s_HN, s_Z, s_XN, s_tr, s_hn, s_tz = (
            sem(n) for n in ("r_product", "hn_product", "z_product", "xn_product", "r_tanh", "hn_copied",
                                   "z_tanh"))
        s_rh, s_npre, s_n, s_hmn, s_zh = (
            sem(n) for n in ("r_times_hn", "n_sum", "n_tanh", "h_minus_n", "z_times"))
        s_hf, s_x2, s_fst, s_fmo, s_fve, s_frs, s_fln, s_fT, s_fTe, s_lg, s_lge, s_top, s_topi = (
            sem(n) for n in ("h_turned_back", "x2_ready", "x2_stats", "x2_moments", "x2_variance",
                                   "x2_rstd", "x2_normed", "ln_turned", "ln_turned_copied",
                                   "logits_product", "logits_copied", "top8_found", "top8_indexed"))

        def nth(l, n):
            return LANES * n + l + 1

        def wait_h(eng, l, n):
            if n % ITERS == 0:
                eng.wait_ge(s_h0, nth(l, n // ITERS))
            else:
                eng.wait_ge(s_h, nth(l, n - 1))

        STAGES = ["prepare"] + ["score", "attend", "gates", "update"] * ITERS + ["finish"]
        SLOTS = len(STAGES) * ROUNDS + LANES - 1

        def at_slot(slot):
            found = {}
            for l in range(LANES):
                r, at = divmod(slot - l, len(STAGES))
                if slot >= l and r < ROUNDS:
                    found[STAGES[at]] = (l, r, ITERS * r + (at - 1) // 4)
            return found

        def num(q, w):
            return q * RB + w

        def turn_of(q, w):
            return q + w // RB

        def wait_pos(eng, s, value):
            if not isinstance(value, int) or value > 0:
                eng.wait_ge(s, value)

        LEAD = 4

        def run_tiles(eng, step):
            last_q = (TILES - 1 - LEAD) // RB

            def plain(j):
                step(j // RB, j % RB, lambda k: 0 <= j + k < TILES)

            for j in range(RB):
                plain(j)
            with eng.Fori(1, last_q) as q:
                for w in range(RB):
                    step(q, w, lambda k: True)
            for j in range(RB * last_q, TILES + 1):
                plain(j)

        block = stack.enter_context(nc.Block())

        @block.sync
        def _(sp):
            sp.dma_start(proj_in[:, :, :], proj).then_inc(s_wload, 16)
            sp.dma_start(col_in[:, :], columns).then_inc(s_wload, 16)
            sp.dma_start(c_in[0][:, :, :], ctx_g[0]).then_inc(s_cload[0], 16)
            sp.dma_start(x_in[0][:, :, :], x_g[0]).then_inc(s_xload[0], 16)
            sp.dma_start(gru_in[:, :, :, :], gru).then_inc(s_gload, 16)
            for l in range(1, LANES):
                sp.dma_start(c_in[l][:, :, :], ctx_g[l]).then_inc(s_cload[l], 16)
                sp.dma_start(x_in[l][:, :, :], x_g[l]).then_inc(s_xload[l], 16)
            sp.dma_start(wg_sb[:, :], Wg).then_inc(s_wmoe, 16)
            sp.dma_start(w1_sb[:, :, 0:F], W1.rearrange("e d f -> d e f")).then_inc(s_wmoe, 16)
            sp.dma_start(w1_sb[:, :, F:], b1).then_inc(s_wmoe, 16)
            sp.dma_start(w2_sb[:, :, :, :], W2.rearrange("e (c p) d -> p e c d", p=P)).then_inc(s_wmoe, 16)
            sp.dma_start(b_in[:, :], b2.rearrange("e (q n) -> (e q) n", q=P // E)).then_inc(s_bload, 16)
            sp.wait_ge(s_bpart, 5)
            for k in range(3):
                sp.dma_start(bias_dram[k, :].rearrange("(p n) -> p n", p=P), b_parts[:, k, :]).then_inc(s_bstore, 16)
            sp.wait_ge(s_bstore, 48)
            sp.wait_ge(s_bzero, 1)
            sp.dma_start(b_rows[0:3, :], bias_dram).then_inc(s_brow, 16)
            sp.wait_ge(s_const, 1)
            ROWS_AT_ONCE = P * (2048 // D)
            for k in range(TOP * T // ROWS_AT_ONCE):
                sp.dma_start(y_dram[k * ROWS_AT_ONCE:(k + 1) * ROWS_AT_ONCE, :].rearrange("(p n) d -> p (n d)", p=P),
                             zeros[:, :]).then_inc(s_yzero, 16)
            for slot in range(SLOTS):
                now = at_slot(slot)
                if "finish" in now:
                    l, r, _ = now["finish"]
                    g = LANES * r + l
                    sp.wait_ge(s_fln, nth(l, r))
                    sp.dma_start(ln_g[g], work[l][:, :, :]).then_inc(s_fst_[l], 16)
                    if r + 1 < ROUNDS:
                        sp.wait_ge(s_x2, nth(l, r))
                        sp.dma_start(x_in[l][:, :, :], x_g[g + LANES]).then_inc(s_xload[l], 16)
                        sp.wait_ge(s_cn, nth(l, r))
                        sp.dma_start(c_in[l][:, :, :], ctx_g[g + LANES]).then_inc(s_cload[l], 16)

            for b in range(RB):
                sp.wait_ge(s_back[b], 16 * len(range(b, TILES, RB)))
            sp.wait_ge(s_yzero, 16 * (TOP * T // ROWS_AT_ONCE))
            y_c = y_dram.rearrange("(c k b s) d -> c k s b d", c=TOP, b=GB, s=P)
            out_g = out.rearrange("(g b) s d -> g s b d", b=GB)

            def load_results(k):
                if k >= LANES:
                    sp.wait_ge(s_both, k - LANES + 1)
                sp.dma_start(x_in[k % LANES][:, :, :], y_c[0, k]).then_inc(s_yload[k % LANES], 16)
                sp.dma_start(c_in[k % LANES][:, :, :], y_c[1, k]).then_inc(s_yload[k % LANES], 16)

            for k in range(LANES):
                load_results(k)
            for k in range(NG):
                sp.wait_ge(s_both, k + 1)
                sp.dma_start(out_g[k], x2[:, GB * k:GB * k + GB, :]).then_inc(s_out, 16)
                if k + LANES < NG:
                    load_results(k + LANES)
            sp.wait_ge(s_out, 16 * NG)

        @block.tensor
        def _(pe):
            pe.wait_ge(s_wload, 32)
            pe.matmul(bank_r[:, 0:P], proj_in[:, 0, :], proj_in[:, 1, :], start=True, stop=True).then_inc(s_wp, 1)
            pe.wait_ge(s_ident, 2)

            def turn(l, src):
                for b in range(GB):
                    last = pe.transpose(lane_bank[l][:, b * P:(b + 1) * P], src[:, b, :], ident[:, :])
                return last

            for slot in range(SLOTS):
                now = at_slot(slot)
                gates = now.get("gates")
                score = now.get("score")
                attend = now.get("attend")
                prepare = now.get("prepare")
                finish = now.get("finish")
                if finish:
                    l, r, _ = finish
                    pe.wait_ge(s_h, nth(l, ITERS * r + ITERS - 1))
                    turn(l, hT[l]).then_inc(s_hf, 1)
                if gates:
                    l, _, n = gates
                    if l or n:
                        pe.wait_ge(s_tr, nth(l, n) - 1)
                    if n == 0:
                        pe.wait_ge(s_we, 4)
                    wait_h(pe, l, n)
                    pe.matmul(bank_r[:, :], whhT[:, 0, :], hT[l][:, :, :], start=True, stop=False)
                if score:
                    l, _, n = score
                    pe.wait_ge(s_sq, nth(l, n))
                    for b in range(GB):
                        last = pe.matmul(lane_bank[l][:, b:b + 1], work[l][:, b, :], ones_col[:, :],
                                         start=True, stop=True)
                    last.then_inc(s_ssq, 1)
                if prepare:
                    l, r, _ = prepare
                    pe.wait_ge(s_cn, nth(l, r))
                    turn(l, work[l]).then_inc(s_cT, 1)
                if gates:
                    l, _, n = gates
                    pe.wait_ge(s_uTe, nth(l, n))
                    pe.matmul(bank_r[:, :], wihT[:, 0, :], uT[l][:, :, :], start=False, stop=True)\
                        .then_inc(s_R, 1)
                if prepare:
                    l, r, _ = prepare
                    pe.wait_ge(s_cTe, nth(l, r))
                    pe.wait_ge(s_we, 3)
                    pe.matmul(lane_bank[l][:, :], wkq[:, :], uT[l][:, :, :], start=True, stop=True)\
                        .then_inc(s_kq, 1)
                if score:
                    l, _, n = score
                    pe.wait_ge(s_ms, nth(l, n))
                    for b in range(GB):
                        last = pe.matmul(lane_bank[l][:, b * P:(b + 1) * P], hT[l][:, b, :], kq[l][:, b, :],
                                         start=True, stop=True)
                    last.then_inc(s_sc, 1)
                if attend:
                    l, _, n = attend
                    pe.wait_ge(s_at, nth(l, n))
                    for b in range(GB):
                        last = pe.matmul(lane_bank[l][:, b:b + 1], prob[l][:, b, :], ones_col[:, :],
                                         start=True, stop=True)
                    last.then_inc(s_as, 1)
                if gates:
                    l, _, n = gates
                    if l or n:
                        pe.wait_ge(s_hn, nth(l, n) - 1)
                    pe.matmul(bank_hn[:, :], whhT[:, 2, :], hT[l][:, :, :], start=True, stop=True)\
                        .then_inc(s_HN, 1)
                if attend:
                    l, _, n = attend
                    pe.wait_ge(s_ase, nth(l, n))
                    for b in range(GB):
                        last = pe.matmul(lane_bank[l][:, b * D:(b + 1) * D], prob[l][:, b, :], v[l][:, b, :],
                                         start=True, stop=True)
                    last.then_inc(s_u, 1)
                if prepare:
                    l, r, _ = prepare
                    pe.wait_ge(s_kqe, nth(l, r))
                    for b in range(GB):
                        last = pe.matmul(lane_bank[l][:, b * D:(b + 1) * D], uT[l][:, b, :], wvT[:, :],
                                         start=True, stop=True)
                    last.then_inc(s_v, 1)
                if score:
                    l, _, n = score
                    pe.wait_ge(s_scs, nth(l, n))
                    turn(l, work[l]).then_inc(s_scT, 1)
                if finish:
                    l, r, _ = finish
                    pe.wait_ge(s_fln, nth(l, r))
                    turn(l, work[l]).then_inc(s_fT, 1)
                if gates:
                    l, _, n = gates
                    if l or n:
                        pe.wait_ge(s_tz, nth(l, n) - 1)
                    pe.matmul(bank_z[:, :], whhT[:, 1, :], hT[l][:, :, :], start=True, stop=False)
                if attend:
                    l, _, n = attend
                    pe.wait_ge(s_un, nth(l, n))
                    turn(l, work[l]).then_inc(s_uT, 1)
                if gates:
                    l, _, n = gates
                    pe.matmul(bank_z[:, :], wihT[:, 1, :], uT[l][:, :, :], start=False, stop=True)\
                        .then_inc(s_Z, 1)
                    if l or n:
                        pe.wait_ge(s_npre, nth(l, n) - 1)
                    pe.matmul(bank_xn[:, :], wihT[:, 2, :], uT[l][:, :, :], start=True, stop=True)\
                        .then_inc(s_XN, 1)
                if prepare:
                    l, r, _ = prepare
                    pe.wait_ge(s_ve, nth(l, r))
                    pe.wait_ge(s_xn_, nth(l, r))
                    turn(l, work[l]).then_inc(s_xT, 1)
                if finish:
                    l, r, _ = finish
                    pe.wait_ge(s_fTe, nth(l, r))
                    pe.wait_ge(s_wmoe, 64)
                    for b in range(GB):
                        last = pe.matmul(lane_bank[l][:, b * E:(b + 1) * E], uT[l][:, b, :], wg_sb[:, :],
                                         start=True, stop=True)
                    last.then_inc(s_lg, 1)

            pe.wait_ge(s_const, 3)
            for c in range(TOP):
                pe.wait_ge(s_mask, c + 1)
                pe.matmul(bank_hid[c][:, 0:E * NTOK], before[:, :], mask[:, c], start=True, stop=True)
                pe.matmul(bank_hid[c][:, E * NTOK:2 * E * NTOK], ones_bf[:, :], mask[:, c],
                          start=True, stop=True).then_inc(s_count, 1)
            table = bank_hn[:, 0:2 * NJ]
            pe.wait_ge(s_iotaf, 5)
            pe.matmul(table, zero_bf[:, 0:P], zero_bf[:, :], start=True, stop=False).then_inc(s_hotuse, 2)
            with pe.Fori(0, NP // 16) as q:
                for b in range(2):
                    pe.wait_ge(s_hot, 2 * q + b + 1)
                    for i in range(8):
                        last = pe.matmul(table, hot_row[b][:, i, :], hot_value[b][:, i, :],
                                         start=False, stop=False)
                    last.then_inc(s_hotuse, 1)
            pe.matmul(table, zero_bf[:, 0:P], zero_bf[:, :], start=False, stop=True).then_inc(s_table, 1)

            pe.wait_ge(s_brow, 16)
            pe.wait_ge(s_texp, 1)

            def turn_rows(q, w):
                pe.wait_ge(s_rows[w % RB], 16 * (turn_of(q, w) + 1))
                wait_pos(pe, s_xe, num(q, w) - 1)
                pe.transpose(bank_rows[w % 2][:, 0:P], rows[w % RB][:, :], ident[:, :]).then_inc(s_xp, 1)

            def first_layer(q, w):
                pe.wait_ge(s_w1, num(q, w) + 1)
                pe.wait_ge(s_xe, num(q, w) + 1)
                wait_pos(pe, s_ge, num(q, w) - 1)
                for c in range(FC):
                    last = pe.matmul(bank_hid[w % 2][:, c * P:(c + 1) * P], w1_now[w % 2][:, c * P:(c + 1) * P],
                                     rowsT[w % 2][:, :], start=True, stop=True)
                last.then_inc(s_hp, 1)

            def second_layer(q, w):
                e = pe.value_load(tile_expert[0:1, bass.ds(num(q, w), 1)], min_val=0, max_val=E - 1)
                pe.wait_ge(s_ge, num(q, w) + 1)
                wait_pos(pe, s_ye, num(q, w) - 1)
                pe.matmul(bank_out[w % 2][:, 0:D], ones_bf[:, :], b_rows[:, bass.ds(e * D, D)],
                          start=True, stop=False)
                for c in range(FC):
                    last = pe.matmul(bank_out[w % 2][:, 0:D], hiddenT[w % 2][:, c, :],
                                     w2_flat[:, bass.ds(e * F + c * D, D)], start=False, stop=(c == FC - 1))
                last.then_inc(s_yp, 1)

            turn_rows(0, 0)
            turn_rows(0, 1)
            first_layer(0, 0)

            def pe_step(q, w, has):
                if has(1):
                    first_layer(q, w + 1)
                if has(2):
                    turn_rows(q, w + 2)
                if has(0):
                    second_layer(q, w)

            run_tiles(pe, pe_step)

        @block.scalar
        def _(act):
            for slot in range(SLOTS):
                now = at_slot(slot)
                gates = now.get("gates")
                score = now.get("score")
                attend = now.get("attend")
                update = now.get("update")
                prepare = now.get("prepare")
                finish = now.get("finish")
                if score:
                    l, r, n = score
                    wait_h(act, l, n)
                    if n == ITERS * r and r:
                        act.wait_ge(s_fst_[l], 16 * r)
                    act.activation(work[l][:, :, :], hT[l][:, :, :], ACT.Square).then_inc(s_sq, 1)
                if prepare:
                    l, r, _ = prepare
                    act.wait_ge(s_cload[l], 16 * (r + 1))
                    for b in range(GB):
                        last = act.activation(prob[l][:, b, :], c_in[l][:, b, :], ACT.Square,
                                              accum_out=csum[l][:, b:b + 1])
                    last.then_inc(s_csq, 1)
                if update:
                    l, _, n = update
                    act.wait_ge(s_npre, nth(l, n))
                    act.activation(tr[l][:, :, :], tr[l][:, :, :], ACT.Tanh, bias=col_in[:, 2:3])\
                        .then_inc(s_n, 1)
                if prepare:
                    l, r, _ = prepare
                    act.wait_ge(s_cT, nth(l, r))
                    act.activation(uT[l][:, :, :], lane_bank[l][:, :], ACT.Copy).then_inc(s_cTe, 1)
                if gates:
                    l, _, n = gates
                    act.wait_ge(s_R, nth(l, n))
                    if n == 0:
                        act.wait_ge(s_bcol, 3)
                    act.activation(tr[l][:, :, :], bank_r[:, :], ACT.Tanh, bias=bias_rz[:, 0:1], scale=0.5)\
                        .then_inc(s_tr, 1)
                    act.wait_ge(s_HN, nth(l, n))
                    act.activation(hn[l][:, :, :], bank_hn[:, :], ACT.Identity, bias=bias_hn[:, :])\
                        .then_inc(s_hn, 1)
                if prepare:
                    l, r, _ = prepare
                    act.wait_ge(s_kq, nth(l, r))
                    act.wait_ge(s_bcol, 3)
                    act.activation(kq[l][:, :, :], lane_bank[l][:, :], ACT.Copy, scale=slot_scale[:, :])\
                        .then_inc(s_kqe, 1)
                if attend:
                    l, _, n = attend
                    act.wait_ge(s_uT, nth(l, n))
                    act.activation(uT[l][:, :, :], lane_bank[l][:, :], ACT.Copy).then_inc(s_uTe, 1)
                if score:
                    l, _, n = score
                    act.wait_ge(s_sub, nth(l, n))
                    act.activation(prob[l][:, :, :], prob[l][:, :, :], ACT.Exp).then_inc(s_exp, 1)
                if gates:
                    l, _, n = gates
                    act.wait_ge(s_Z, nth(l, n))
                    act.activation(tz[l][:, :, :], bank_z[:, :], ACT.Tanh, bias=bias_rz[:, 1:2], scale=0.5)\
                        .then_inc(s_tz, 1)
                if finish:
                    l, r, _ = finish
                    act.wait_ge(s_fT, nth(l, r))
                    act.activation(uT[l][:, :, :], lane_bank[l][:, :], ACT.Copy).then_inc(s_fTe, 1)
                if prepare:
                    l, r, _ = prepare
                    act.wait_ge(s_xT, nth(l, r))
                    act.activation(hT[l][:, :, :], lane_bank[l][:, :], ACT.Copy).then_inc(s_h0, 1)

            act.wait_ge(s_shift, 2)
            act.activation(exps[:, :, :], exps[:, :, :], ACT.Exp).then_inc(s_gexp, 1)
            act.activation(exp2[:, :], exp2[:, :], ACT.Exp).then_inc(s_gexp, 1)

            def copy_rows(q, w):
                act.wait_ge(s_xp, num(q, w) + 1)
                wait_pos(act, s_hp, num(q, w) - 1)
                act.activation(rowsT[w % 2][:, :], bank_rows[w % 2][:, 0:P], ACT.Copy).then_inc(s_xe, 1)

            def gelu(q, w):
                act.wait_ge(s_hp, num(q, w) + 1)
                wait_pos(act, s_yp, num(q, w) - 1)
                for c in range(FC):
                    last = act.activation(hiddenT[w % 2][:, c, :], bank_hid[w % 2][:, c * P:(c + 1) * P], ACT.Gelu,
                                          bias=w1_now[w % 2][:, F + c:F + c + 1])
                last.then_inc(s_ge, 1)

            copy_rows(0, 0)
            copy_rows(0, 1)

            def act_step(q, w, has):
                if has(0):
                    gelu(q, w)
                if has(2):
                    copy_rows(q, w + 2)

            run_tiles(act, act_step)

        @block.vector
        def _(dve):
            def spread(column):
                return column[:, :].unsqueeze(2).to_broadcast([P, GB, P])

            def bank3(bank):
                return bank[:, :].rearrange("p (b s) -> p b s", b=GB)

            dve.wait_ge(s_wload, 32)
            dve.tensor_tensor(bias_rz[:, :], col_in[:, 0:2], col_in[:, 3:5], ALU.add).then_inc(s_we, 1)
            dve.wait_ge(s_we, 1)
            dve.tensor_scalar(bias_rz[:, :], bias_rz[:, :], 0.5, None, ALU.mult).then_inc(s_bcol, 1)
            dve.tensor_scalar(bias_hn[:, :], col_in[:, 5:6], 0.5, None, ALU.mult).then_inc(s_bcol, 1)
            dve.tensor_scalar(slot_scale[:, :], col_in[:, 6:7], SCALE, None, ALU.mult).then_inc(s_bcol, 1)
            dve.tensor_scalar(wvT[:, :], proj_in[:, 2, :], col_in[:, 7:8], None, ALU.mult).then_inc(s_we, 1)
            dve.wait_ge(s_wp, 1)
            dve.tensor_scalar(wkq[:, :], bank_r[:, 0:P], col_in[:, 7:8], None, ALU.mult).then_inc(s_we, 1)
            dve.wait_ge(s_gload, 16)
            dve.tensor_scalar(whhT[:, 2, :], whhT[:, 2, :], 0.5, None, ALU.mult).then_inc(s_we, 1)

            def bias_parts():
                dve.wait_ge(s_bload, 16)
                dve.tensor_copy(b_parts[:, 0, :], b_in[:, :]).then_inc(s_bpart, 1)
                dve.wait_ge(s_bpart, 1)
                dve.tensor_tensor(b_rest[:, 0, :], b_in[:, :], b_parts[:, 0, :], ALU.subtract).then_inc(s_bpart, 1)
                dve.wait_ge(s_bpart, 2)
                dve.tensor_copy(b_parts[:, 1, :], b_rest[:, 0, :]).then_inc(s_bpart, 1)
                dve.wait_ge(s_bpart, 3)
                dve.tensor_tensor(b_rest[:, 1, :], b_rest[:, 0, :], b_parts[:, 1, :], ALU.subtract)\
                    .then_inc(s_bpart, 1)
                dve.wait_ge(s_bpart, 4)
                dve.tensor_copy(b_parts[:, 2, :], b_rest[:, 1, :]).then_inc(s_bpart, 1)

            def moments_of(src, l, times, st, mo, ve):
                for b in range(GB):
                    last = dve.bn_stats(stats[l][:, b, :], src(b))
                last.then_inc(st, 1)
                dve.wait_ge(st, times)
                for b in range(GB):
                    last = dve.bn_aggr(moments[l][:, b, :], stats[l][:, b, :])
                last.then_inc(mo, 1)
                dve.wait_ge(mo, times)
                dve.tensor_scalar(rstd[l][:, :], moments[l][:, :, 1], 1e-5, None, ALU.add).then_inc(ve, 1)

            def normed(src, l, done):
                for b in range(GB):
                    last = dve.tensor_scalar(work[l][:, b, :], src(b), moments[l][:, b, 0:1],
                                             rstd[l][:, b:b + 1], ALU.subtract, ALU.mult)
                last.then_inc(done, 1)

            for slot in range(SLOTS):
                now = at_slot(slot)
                score = now.get("score")
                attend = now.get("attend")
                update = now.get("update")
                prepare = now.get("prepare")
                finish = now.get("finish")
                if slot == 6:
                    bias_parts()
                if attend:
                    l, _, n = attend
                    dve.wait_ge(s_exp, nth(l, n))
                    dve.tensor_reduce(zsum[l][:, :], prob[l][:, :, :], AX.X, ALU.add).then_inc(s_zs, 1)
                    dve.wait_ge(s_zs, nth(l, n))
                    dve.reciprocal(zinv[l][:, :], zsum[l][:, :]).then_inc(s_zi, 1)
                if score:
                    l, _, n = score
                    dve.wait_ge(s_ssq, nth(l, n))
                    dve.tensor_scalar(rms[l][:, :], lane_bank[l][:, 0:GB], 1.0 / D, 1e-6, ALU.mult, ALU.add)\
                        .then_inc(s_ms, 1)
                if prepare:
                    l, r, _ = prepare
                    dve.wait_ge(s_csq, nth(l, r))
                    dve.tensor_scalar(crms[l][:, :], csum[l][:, :], 1.0 / D, 1e-6, ALU.mult, ALU.add)\
                        .then_inc(s_cms, 1)
                if finish:
                    l, r, _ = finish
                    g = LANES * r + l
                    dve.wait_ge(s_hf, nth(l, r))
                    dve.tensor_tensor(x2[:, GB * g:GB * g + GB, :], bank3(lane_bank[l]), x_in[l][:, :, :],
                                      ALU.add).then_inc(s_x2, 1)
                if update:
                    l, _, n = update
                    dve.wait_ge(s_tr, nth(l, n))
                    dve.wait_ge(s_hn, nth(l, n))
                    dve.scalar_tensor_tensor(tr[l][:, :, :], tr[l][:, :, :], 1.0, hn[l][:, :, :],
                                             ALU.add, ALU.mult).then_inc(s_rh, 1)
                    dve.wait_ge(s_rh, nth(l, n))
                    dve.wait_ge(s_XN, nth(l, n))
                    dve.tensor_tensor(tr[l][:, :, :], tr[l][:, :, :], bank3(bank_xn), ALU.add)\
                        .then_inc(s_npre, 1)
                if prepare:
                    l, r, _ = prepare
                    dve.wait_ge(s_crms, nth(l, r))
                    if r:
                        dve.wait_ge(s_fst_[l], 16 * r)
                    dve.tensor_tensor(work[l][:, :, :], c_in[l][:, :, :], spread(crms[l]), ALU.mult)\
                        .then_inc(s_cn, 1)
                    dve.wait_ge(s_xload[l], 16 * (r + 1))
                    moments_of(lambda b: x_in[l][:, b, :], l, nth(l, r), s_xst, s_xmo, s_xve)
                if finish:
                    l, r, _ = finish
                    g = LANES * r + l
                    dve.wait_ge(s_x2, nth(l, r))
                    moments_of(lambda b: x2[:, GB * g + b, :], l, nth(l, r), s_fst, s_fmo, s_fve)
                if score:
                    l, _, n = score
                    dve.wait_ge(s_sc, nth(l, n))
                    dve.wait_ge(s_rms, nth(l, n))
                    dve.tensor_tensor(work[l][:, :, :], bank3(lane_bank[l]), spread(rms[l]), ALU.mult)\
                        .then_inc(s_scs, 1)
                if attend:
                    l, _, n = attend
                    dve.wait_ge(s_as, nth(l, n))
                    dve.tensor_scalar(asum[l][:, :], lane_bank[l][:, 0:GB], 1e-6, None, ALU.add)\
                        .then_inc(s_ase, 1)
                    dve.wait_ge(s_ase, nth(l, n))
                    dve.reciprocal(ainv[l][:, :], asum[l][:, :]).then_inc(s_ai, 1)
                if finish:
                    l, r, _ = finish
                    dve.wait_ge(s_frs, nth(l, r))
                    normed(lambda b: x2[:, GB * g + b, :], l, s_fln)
                if update:
                    l, _, n = update
                    dve.wait_ge(s_hmn, nth(l, n))
                    dve.wait_ge(s_tz, nth(l, n))
                    dve.scalar_tensor_tensor(hn[l][:, :, :], tz[l][:, :, :], 1.0, hn[l][:, :, :],
                                             ALU.add, ALU.mult).then_inc(s_zh, 1)
                    dve.wait_ge(s_zh, nth(l, n))
                    dve.scalar_tensor_tensor(hT[l][:, :, :], hn[l][:, :, :], 0.5, tr[l][:, :, :],
                                             ALU.mult, ALU.add).then_inc(s_h, 1)
                if attend:
                    l, _, n = attend
                    dve.wait_ge(s_ai, nth(l, n))
                    dve.wait_ge(s_u, nth(l, n))
                    dve.tensor_tensor(work[l][:, :, :], bank3(lane_bank[l]), spread(ainv[l]), ALU.mult)\
                        .then_inc(s_un, 1)
                if prepare:
                    l, r, _ = prepare
                    dve.wait_ge(s_v, nth(l, r))
                    dve.tensor_copy(v[l][:, :, :], bank3(lane_bank[l])).then_inc(s_ve, 1)
                    dve.wait_ge(s_xrs, nth(l, r))
                    normed(lambda b: x_in[l][:, b, :], l, s_xn_)
                if score:
                    l, _, n = score
                    dve.wait_ge(s_scT, nth(l, n))
                    dve.tensor_reduce(peak[l][:, :], bank3(lane_bank[l]), AX.X, ALU.max).then_inc(s_pk, 1)
                    dve.wait_ge(s_pk, nth(l, n))
                    dve.tensor_tensor(prob[l][:, :, :], bank3(lane_bank[l]), spread(peak[l]), ALU.subtract)\
                        .then_inc(s_sub, 1)
                if finish:
                    l, r, _ = finish
                    g = LANES * r + l
                    dve.wait_ge(s_lg, nth(l, r))
                    tiles = slice(GB * g, GB * g + GB)
                    dve.tensor_copy(logits[:, tiles, :],
                                    lane_bank[l][:, 0:GB * E].rearrange("p (b e) -> p b e", b=GB))\
                        .then_inc(s_lge, 1)
                    dve.wait_ge(s_lge, nth(l, r))
                    for b in range(GB):
                        last = dve.max(top8[:, GB * g + b, :], logits[:, GB * g + b, :])
                    last.then_inc(s_top, 1)
                    dve.wait_ge(s_top, nth(l, r))
                    for b in range(GB):
                        last = dve.max_index(top8_at[:, GB * g + b, :], top8[:, GB * g + b, :],
                                             logits[:, GB * g + b, :])
                    last.then_inc(s_topi, 1)

            steps = [0]

            def link(ins):
                steps[0] += 1
                ins.then_inc(s_route, 1)
                dve.wait_ge(s_route, steps[0])

            def per_token(t):
                return t.unsqueeze(1).to_broadcast([P, E, NTOK])

            def per_expert(t):
                return t.unsqueeze(2).to_broadcast([P, E, NTOK])

            dve.wait_ge(s_topi, NG)
            dve.wait_ge(s_iotaf, 5)
            for c in range(TOP):
                link(dve.tensor_copy(at[:, c, :], top8_at[:, :, c]))
            for c in range(TOP):
                dve.tensor_tensor(mask[:, c], per_token(at[:, c, :]), per_expert(iota_f[:, 0:E]), ALU.is_equal)\
                    .then_inc(s_mask, 1)
            dve.tensor_tensor(exps[:, :, :], logits[:, :, :], top8[:, :, 0:1].to_broadcast([P, NTOK, E]),
                              ALU.subtract).then_inc(s_shift, 1)
            dve.tensor_tensor(exp2[:, :], top8[:, :, 1], top8[:, :, 0], ALU.subtract).then_inc(s_shift, 1)
            dve.wait_ge(s_mask, 2)
            for c in range(TOP):
                in_tile_count = bank_hid[c][:, 0:E * NTOK].rearrange("p (e t) -> p e t", e=E)
                total = bank_hid[c][:, E * NTOK:2 * E * NTOK]
                flat = upto[:, c].rearrange("p e t -> p (e t)")
                dve.wait_ge(s_count, c + 1)
                link(dve.tensor_tensor_scan(flat, restart[:, :, :].rearrange("p e t -> p (e t)"), total, 0.0,
                                            ALU.mult, ALU.add))
                link(dve.tensor_tensor(place[:, c], upto[:, c], total.rearrange("p (e t) -> p e t", e=E),
                                       ALU.subtract))
                link(dve.tensor_tensor(place[:, c], place[:, c], in_tile_count, ALU.add))
                if c:
                    link(dve.tensor_tensor(place[:, c], place[:, c], per_expert(upto[:, 0, :, NTOK - 1]), ALU.add))
                link(dve.tensor_tensor(place[:, c], place[:, c], mask[:, c], ALU.mult))
                link(dve.tensor_reduce(pos[:, c, :], place[:, c].rearrange("p e t -> p t e"), AX.X, ALU.add))
            link(dve.tensor_scalar(keep[:, :, :], pos[:, :, :], float(CAP), None, ALU.is_lt))
            link(dve.tensor_scalar(pos[:, :, :], pos[:, :, :], float(CAP - 1), None, ALU.min))
            link(dve.tensor_tensor(filled[:, :], upto[:, 0, :, NTOK - 1], upto[:, 1, :, NTOK - 1], ALU.add))
            link(dve.tensor_scalar(filled[:, :], filled[:, :], float(CAP), None, ALU.min))
            link(dve.tensor_tensor(compare[:, 0:E, :], filled[:, :].unsqueeze(2).to_broadcast([P, E, QS]),
                                   steps128[:, :].unsqueeze(1).to_broadcast([P, E, QS]), ALU.is_gt))
            link(dve.tensor_reduce(tiles_of[:, :], compare[:, 0:E, :], AX.X, ALU.add))
            link(dve.tensor_tensor_scan(tile_end[:, :], restart[:, 0, 1:1 + E], tiles_of[:, :], 0.0,
                                        ALU.mult, ALU.add))
            link(dve.tensor_tensor(tile_base[:, :], tile_end[:, :], tiles_of[:, :], ALU.subtract))
            for c in range(TOP):
                link(dve.tensor_tensor(place[:, c], mask[:, c], per_expert(tile_base[:, :]), ALU.mult))
                link(dve.tensor_reduce(base_of[:, c, :], place[:, c].rearrange("p e t -> p t e"), AX.X, ALU.add))
            pos_f = pos[:, :, :].rearrange("p c t -> p (c t)")
            depth_f = depth[:, :, :].rearrange("p c t -> p (c t)")
            link(dve.tensor_tensor(compare[:, :, :], pos_f.unsqueeze(2).to_broadcast([P, NP, QS]),
                                   steps128[:, :].unsqueeze(1).to_broadcast([P, NP, QS]), ALU.is_ge))
            link(dve.tensor_reduce(depth_f, compare[:, :, :], AX.X, ALU.add))
            link(dve.scalar_tensor_tensor(in_tile[:, :], depth_f, -float(P), pos_f, ALU.mult, ALU.add))
            link(dve.tensor_scalar(in_tile[:, :], in_tile[:, :], float(P), None, ALU.add))
            link(dve.tensor_tensor(which[:, :], depth_f, base_of[:, :, :].rearrange("p c t -> p (c t)"), ALU.add))
            link(dve.tensor_scalar(pos[:, :, :], keep[:, :, :], -1000.0, 999.0, ALU.mult, ALU.add))
            link(dve.tensor_tensor(which[:, :], which[:, :], pos_f, ALU.add))
            with dve.Fori(0, NP // 16) as q:
                for b in range(2):
                    pairs = bass.ds(16 * q + 8 * b, 8)
                    dve.wait_ge(s_hotuse, 2 * q + b + 1)
                    dve.tensor_tensor(hot_row[b][:, :, :], in_tile[:, pairs].unsqueeze(2).to_broadcast([P, 8, P]),
                                      iota_f[:, :].unsqueeze(1).to_broadcast([P, 8, P]), ALU.is_equal)
                    dve.tensor_tensor(hot_tile[b][:, :, :], which[:, pairs].unsqueeze(2).to_broadcast([P, 8, NJ]),
                                      iota_f[:, 0:NJ].unsqueeze(1).to_broadcast([P, 8, NJ]), ALU.is_equal)\
                        .then_inc(s_hott, 1)
                    dve.wait_ge(s_hott, 2 * q + b + 1)
                    dve.tensor_tensor(hot_value[b][:, :, 0:NJ], hot_tile[b][:, :, :],
                                      iota_f[:, bass.ds(16 * q + 8 * b + 1, 8)].unsqueeze(2)
                                      .to_broadcast([P, 8, NJ]), ALU.mult)
                    dve.tensor_scalar(hot_value[b][:, :, NJ:2 * NJ], hot_tile[b][:, :, :], row_f[:, :], None,
                                      ALU.mult).then_inc(s_hot, 1)
            dve.tensor_tensor(ended[:, :, :], tile_end[0:1, :].unsqueeze(1).to_broadcast([1, NJ, E]),
                              iota_f[0:1, 0:NJ].unsqueeze(2).to_broadcast([1, NJ, E]), ALU.is_le)\
                .then_inc(s_gate, 1)
            dve.wait_ge(s_gate, 1)
            dve.tensor_reduce(tile_expert_f[:, :], ended[:, :, :], AX.X, ALU.add).then_inc(s_gate, 1)
            dve.wait_ge(s_gate, 2)
            dve.tensor_scalar(tile_expert[:, :], tile_expert_f[:, :], float(E - 1), None, ALU.min)\
                .then_inc(s_texp, 1)
            table_tile, table_row = bank_hn[:, 0:NJ], bank_hn[:, NJ:2 * NJ]
            dve.wait_ge(s_table, 1)
            link(dve.tensor_scalar(rows_f[:, :], table_tile, float(P), -float(P), ALU.mult, ALU.add))
            link(dve.tensor_tensor(rows_f[:, :], rows_f[:, :], table_row, ALU.add))
            link(dve.tensor_scalar(rows_g[:, :], rows_f[:, :], float(T), -float(T), ALU.is_ge, ALU.mult))
            link(dve.tensor_tensor(rows_g[:, :], rows_g[:, :], rows_f[:, :], ALU.add))
            link(dve.tensor_scalar(from_rows[:, :], rows_g[:, :], 0.0, None, ALU.max))
            link(dve.tensor_scalar(rows_e[:, :], table_tile, 0.0, INVALID, ALU.is_equal, ALU.mult))
            link(dve.tensor_tensor(to_rows[:, :], rows_f[:, :], rows_e[:, :], ALU.add))

            def from_column(q, w):
                if not (isinstance(q, int) and turn_of(q, w) == 0):
                    dve.wait_ge(s_rows[w % RB], 16 * turn_of(q, w))
                dve.tensor_copy(from_col[w % RB][:, :], from_rows[:, bass.ds(num(q, w), 1)]).then_inc(s_fcol, 1)

            def to_column(q, w):
                if not (isinstance(q, int) and turn_of(q, w) == 0):
                    dve.wait_ge(s_back[w % RB], 16 * turn_of(q, w))
                dve.tensor_copy(to_col[w % RB][:, :], to_rows[:, bass.ds(num(q, w), 1)]).then_inc(s_tcol, 1)

            def copy_w1(q, w):
                e = dve.value_load(tile_expert[0:1, bass.ds(num(q, w), 1)], min_val=0, max_val=E - 1)
                wait_pos(dve, s_ge, num(q, w) - 1)
                wait_pos(dve, s_hp, num(q, w) - 1)
                dve.tensor_copy(w1_now[w % 2][:, :], w1_flat[:, bass.ds(e * (F + FC), F + FC)]).then_inc(s_w1, 1)

            def copy_results(q, w):
                dve.wait_ge(s_yp, num(q, w) + 1)
                dve.tensor_copy(results[w % RB][:, :], bank_out[w % 2][:, 0:D]).then_inc(s_ye, 1)

            for j in range(LEAD):
                from_column(0, j)
            dve.wait_ge(s_texp, 1)
            for j in range(2):
                copy_w1(0, j)
            dve.wait_ge(s_gexp, 2)
            gsteps = [2]

            def glink(ins):
                gsteps[0] += 1
                ins.then_inc(s_gate, 1)
                dve.wait_ge(s_gate, gsteps[0])

            glink(dve.tensor_reduce(gsum[:, :], exps[:, :, :], AX.X, ALU.add))
            glink(dve.reciprocal(gate[0][:, :], gsum[:, :]))
            glink(dve.tensor_tensor(gate[1][:, :], gate[0][:, :], exp2[:, :], ALU.mult))
            glink(dve.scalar_tensor_tensor(denom[:, :], gate[0][:, :], 1e-9, gate[1][:, :], ALU.add, ALU.add))
            glink(dve.reciprocal(gsum[:, :], denom[:, :]))
            for c in range(TOP):
                glink(dve.tensor_tensor(gate[c][:, :], gate[c][:, :], gsum[:, :], ALU.mult))
                glink(dve.tensor_tensor(gate[c][:, :], gate[c][:, :], keep[:, c, :], ALU.mult))

            def dve_step(q, w, has):
                if has(LEAD):
                    from_column(q, w + LEAD)
                if has(2):
                    copy_w1(q, w + 2)
                if has(0):
                    to_column(q, w)
                    copy_results(q, w)

            run_tiles(dve, dve_step)

            for k in range(NG):
                dve.wait_ge(s_yload[k % LANES], 32 * (k // LANES + 1))
                for c, y in enumerate((x_in[k % LANES], c_in[k % LANES])):
                    if c:
                        dve.wait_ge(s_first, k + 1)
                    for b in range(GB):
                        t = GB * k + b
                        last = dve.scalar_tensor_tensor(x2[:, t, :], y[:, b, :], gate[c][:, t:t + 1], x2[:, t, :],
                                                        ALU.mult, ALU.add)
                    last.then_inc(s_both if c else s_first, 1)

        @block.gpsimd
        def _(pool):
            pool.memset(ident[:, :], 0.0).then_inc(s_ident, 1)
            pool.memset(ones_col[:, :], 1.0)
            pool.memset(neg_half[:, :], -0.5)
            pool.wait_ge(s_ident, 1)
            pool.affine_select(out=ident[:, :], in_=ident[:, :], compare_op=ALU.not_equal, fill=1.0, base=0,
                               pattern=[[-1, P]], channel_multiplier=1).then_inc(s_ident, 1)
            pool.memset(zeros[:, :], 0.0).then_inc(s_const, 1)
            pool.memset(b_rows[:, :], 0.0).then_inc(s_bzero, 1)
            pool.memset(ones_bf[:, :], 1.0).then_inc(s_const, 1)
            pool.wait_ge(s_const, 2)
            pool.affine_select(out=before[:, :], in_=ones_bf[:, :], compare_op=ALU.is_gt, fill=0.0, base=0,
                               pattern=[[1, P]], channel_multiplier=-1).then_inc(s_const, 1)
            pool.iota(iota_i[:, :], [[1, P]], base=0, channel_multiplier=0).then_inc(s_iota, 1)
            pool.iota(row_i[:, :], [[1, 1]], base=0, channel_multiplier=1).then_inc(s_iota, 1)
            pool.memset(restart[:, :, :], 1.0).then_inc(s_iota, 1)
            pool.memset(zero_bf[:, :], 0.0).then_inc(s_iotaf, 1)
            pool.wait_ge(s_iota, 3)
            pool.tensor_copy(iota_f[:, :], iota_i[:, :]).then_inc(s_iotaf, 1)
            pool.tensor_copy(row_f[:, :], row_i[:, :]).then_inc(s_iotaf, 1)
            pool.memset(restart[:, :, 0:1], 0.0).then_inc(s_iotaf, 1)
            pool.wait_ge(s_iotaf, 4)
            pool.tensor_scalar(steps128[:, :], iota_f[:, 0:QS], float(P), None, ALU.mult).then_inc(s_iotaf, 1)
            for slot in range(SLOTS):
                now = at_slot(slot)
                if "prepare" in now:
                    l, r, _ = now["prepare"]
                    pool.wait_ge(s_cms, nth(l, r))
                    pool.tensor_tensor(crms[l][:, :], crms[l][:, :], neg_half[:, :], ALU.pow).then_inc(s_crms, 1)
                if "attend" in now:
                    l, _, n = now["attend"]
                    pool.wait_ge(s_zi, nth(l, n))
                    pool.tensor_tensor(prob[l][:, :, :], prob[l][:, :, :],
                                       zinv[l][:, :].unsqueeze(2).to_broadcast([P, GB, P]), ALU.mult)\
                        .then_inc(s_at, 1)
                if "score" in now:
                    l, _, n = now["score"]
                    pool.wait_ge(s_ms, nth(l, n))
                    pool.tensor_tensor(rms[l][:, :], rms[l][:, :], neg_half[:, :], ALU.pow).then_inc(s_rms, 1)
                if "prepare" in now:
                    l, r, _ = now["prepare"]
                    pool.wait_ge(s_xve, nth(l, r))
                    pool.tensor_tensor(rstd[l][:, :], rstd[l][:, :], neg_half[:, :], ALU.pow).then_inc(s_xrs, 1)
                if "finish" in now:
                    l, r, _ = now["finish"]
                    pool.wait_ge(s_fve, nth(l, r))
                    pool.tensor_tensor(rstd[l][:, :], rstd[l][:, :], neg_half[:, :], ALU.pow).then_inc(s_frs, 1)
                if "update" in now:
                    l, _, n = now["update"]
                    pool.wait_ge(s_n, nth(l, n))
                    pool.tensor_tensor(hn[l][:, :, :], hT[l][:, :, :], tr[l][:, :, :], ALU.subtract)\
                        .then_inc(s_hmn, 1)

            for l in range(LANES):
                pool.wait_ge(s_fst_[l], 16 * ROUNDS)
            pool.wait_ge(s_yzero, 16 * (TOP * T // (P * (2048 // D))))

            def gather(q, w):
                pool.wait_ge(s_fcol, num(q, w) + 1)
                wait_pos(pool, s_xp, num(q, w) - RB + 1)
                pool.sem_inc(s_go, 1)
                pool.indirect_dma_start(rows[w % RB][:, :], None, ln_dram,
                                        bass.IndirectOffsetOnAxis(ap=from_col[w % RB][:, 0:1], axis=0))\
                    .then_inc(s_rows[w % RB], 16)

            def scatter(q, w):
                pool.wait_ge(s_tcol, num(q, w) + 1)
                pool.wait_ge(s_ye, num(q, w) + 1)
                pool.sem_inc(s_go, 1)
                pool.indirect_dma_start(y_dram, bass.IndirectOffsetOnAxis(ap=to_col[w % RB][:, 0:1], axis=0),
                                        results[w % RB][:, :], None, bounds_check=TOP * T - 1, oob_is_err=False)\
                    .then_inc(s_back[w % RB], 16)

            for j in range(LEAD):
                gather(0, j)

            def pool_step(q, w, has):
                if has(LEAD):
                    gather(q, w + LEAD)
                if has(0):
                    scatter(q, w)

            run_tiles(pool, pool_step)



def kernel(**inputs):
    import numpy as _np
    import concourse.bacc as _bacc
    from concourse import mybir as _mybir
    from concourse.bass_utils import run_bass_kernel_spmd as _run

    nc = _bacc.Bacc("TRN2", target_bir_lowering=False, num_devices=1)
    arrays, args = {}, []
    w = {k.removeprefix("L0_").removeprefix("xattn_").removeprefix("ffn_"): _np.asarray(a) for k, a in inputs.items()}
    D = w["Wq"].shape[0]

    def turned(m):
        return m.reshape(3, D, D).transpose(2, 0, 1)

    laid_out = {
        "x": w["x"], "ctx": w["ctx_1024"],
        "proj": _np.stack([w["Wk"], w["Wq"], w["Wv"].T], axis=1),
        "gru": _np.stack([turned(w["gru_wih"]), turned(w["gru_whh"])], axis=1),
        "columns": _np.concatenate([w["gru_bih"].reshape(3, D), w["gru_bhh"].reshape(3, D),
                                    w["slot_norm_w"][None], w["input_norm_w"][None]]).T,
        "Wg": w["Wg"], "W1": w["W1"], "b1": w["b1"].reshape(len(w["b1"]), -1, 128).transpose(2, 0, 1), "W2": w["W2"], "b2": w["b2"],
    }
    for name, a in laid_out.items():
        a = _np.ascontiguousarray(a)
        arrays[f"in_{name}"] = a
        args.append(nc.dram_tensor(f"in_{name}", a.shape, _mybir.dt.from_np(a.dtype), kind="ExternalInput").ap())
    out = nc.dram_tensor("out_0", tuple(inputs["x"].shape), F32, kind="ExternalOutput").ap()
    xattn_moe_kernel(nc, *args, out)
    r = _run(nc, [arrays], core_ids=[0])
    return r.results[0]["out_0"]
```

```python
from contextlib import ExitStack

import concourse.bass as bass
from concourse import mybir

F32 = mybir.dt.float32
BF16 = mybir.dt.bfloat16
U32 = mybir.dt.uint32
I32 = mybir.dt.int32
ALU = mybir.AluOpType
ACT = mybir.ActivationFunctionType
AX = mybir.AxisListType

P = 128


def xattn_moe_kernel(nc, x, ctx, proj, gru, columns, Wg, W1, b1, W2, b2, out):
    B, S, D = x.shape
    E, _, F = W1.shape
    TOP = 2
    T = B * S
    CAP = 2 * TOP * T // E
    NTOK = T // P
    GB = 4
    NG = B // GB
    LANES = 4
    ROUNDS = NG // LANES
    ITERS = 3
    GW = GB * S
    FC = F // P
    TILES = TOP * T // P + E - 1
    NJ = TILES + TILES % 2
    SCALE = float(D) ** -0.5
    QS = CAP // P
    INVALID = 16384.0

    ln_dram = nc.dram_tensor("ln_rows", [T, D], F32, kind="Internal").ap()
    y_dram = nc.dram_tensor("expert_rows", [TOP * T, D], F32, kind="Internal").ap()
    bias_dram = nc.dram_tensor("bias_parts", [3, E * D], BF16, kind="Internal").ap()

    x_g = x.rearrange("(g b) s d -> g s b d", b=GB)
    ctx_g = ctx.rearrange("(g b) s d -> g s b d", b=GB)
    ln_g = ln_dram.rearrange("(g b s) d -> g s b d", b=GB, s=S)

    with ExitStack() as stack:
        def sb(name, shape, dt=F32):
            return stack.enter_context(nc.sbuf_tensor(name, shape, dt))

        def psum(name):
            return stack.enter_context(nc.psum_tensor(name, [P, 512], F32))

        def sem(name):
            return stack.enter_context(nc.semaphore(name))

        def lane_sems(name):
            return [sem(f"{name}{l}") for l in range(LANES)]

        ident = sb("ident", [P, P])
        ones_col = sb("ones_col", [P, 1])
        ones_bf = sb("ones_bf", [P, P], BF16)
        before = sb("before", [P, P], BF16)
        zeros = sb("zeros", [P, 2048])
        neg_half = sb("neg_half", [P, GB])
        proj_in = sb("proj_in", [P, 3, D])
        gru_in = sb("gru_in", [P, 2, 3, D])
        col_in = sb("col_in", [P, 8])
        wkq = sb("wkq", [P, D])
        wvT = sb("wvT", [P, D])
        wihT = gru_in[:, 0]
        whhT = gru_in[:, 1]
        bias_rz = sb("bias_rz", [P, 2])
        bias_hn = sb("bias_hn", [P, 1])
        slot_scale = sb("slot_scale", [P, 1])
        wg_sb = sb("wg_sb", [P, E])
        w1_sb = sb("w1_sb", [P, E, F + FC])
        w2_sb = sb("w2_sb", [P, E, FC, D])
        w1_now = [sb(f"w1_now{b}", [P, F + FC]) for b in range(2)]
        b_in = sb("b_in", [P, E * D // P])
        b_parts = sb("b_parts", [P, 3, E * D // P], BF16)
        b_rest = sb("b_rest", [P, 2, E * D // P])
        b_rows = sb("b_rows", [P, E * D], BF16)
        w1_flat = w1_sb[:, :, :].rearrange("p e f -> p (e f)")
        w2_flat = w2_sb[:, :, :, :].rearrange("p e c d -> p (e c d)")

        c_in = [sb(f"c_in{l}", [P, GB, D]) for l in range(LANES)]
        hT = [sb(f"hT{l}", [P, GB, S]) for l in range(LANES)]
        work = [sb(f"work{l}", [P, GB, P]) for l in range(LANES)]
        prob = [sb(f"prob{l}", [P, GB, S]) for l in range(LANES)]
        uT = [sb(f"uT{l}", [P, GB, S]) for l in range(LANES)]
        tr = [sb(f"tr{l}", [P, GB, S]) for l in range(LANES)]
        tz = [sb(f"tz{l}", [P, GB, S]) for l in range(LANES)]
        hn = [sb(f"hn{l}", [P, GB, S]) for l in range(LANES)]
        kq = [sb(f"kq{l}", [P, GB, P]) for l in range(LANES)]
        v = [sb(f"v{l}", [P, GB, D + 1]) for l in range(LANES)]
        rms = [sb(f"rms{l}", [P, GB]) for l in range(LANES)]
        peak = [sb(f"peak{l}", [P, GB]) for l in range(LANES)]
        zsum = [sb(f"zsum{l}", [P, GB]) for l in range(LANES)]
        zinv = [sb(f"zinv{l}", [P, GB]) for l in range(LANES)]
        asum = [sb(f"asum{l}", [P, GB]) for l in range(LANES)]
        ainv = [sb(f"ainv{l}", [P, GB]) for l in range(LANES)]
        stats = [sb(f"stats{l}", [P, GB, 6]) for l in range(LANES)]
        moments = [sb(f"moments{l}", [P, GB, 2]) for l in range(LANES)]
        rstd = [sb(f"rstd{l}", [P, GB]) for l in range(LANES)]
        csum = [sb(f"csum{l}", [P, GB]) for l in range(LANES)]
        crms = [sb(f"crms{l}", [P, GB]) for l in range(LANES)]

        x2 = sb("x2", [P, NTOK, D])
        logits = sb("logits", [P, NTOK, E])
        top8 = sb("top8", [P, NTOK, E])
        top8_at = sb("top8_at", [P, NTOK, E], U32)

        NP = TOP * NTOK
        iota_i = sb("iota_i", [P, P], I32)
        iota_f = sb("iota_f", [P, P])
        row_i = sb("row_i", [P, 1], I32)
        row_f = sb("row_f", [P, 1])
        steps128 = sb("steps128", [P, QS])
        restart = sb("restart", [P, E, NTOK])
        at = sb("at", [P, TOP, NTOK])
        mask = sb("mask", [P, TOP, E, NTOK], BF16)
        upto = sb("upto", [P, TOP, E, NTOK])
        place = sb("place", [P, TOP, E, NTOK])
        pos = sb("pos", [P, TOP, NTOK])
        keep = sb("keep", [P, TOP, NTOK])
        filled = sb("filled", [P, E])
        compare = sb("compare", [P, NP, QS])
        tiles_of = sb("tiles_of", [P, E])
        tile_end = sb("tile_end", [P, E])
        tile_base = sb("tile_base", [P, E])
        base_of = sb("base_of", [P, TOP, NTOK])
        depth = sb("depth", [P, TOP, NTOK])
        in_tile = sb("in_tile", [P, NP])
        which = sb("which", [P, NP])
        hot_row = [sb(f"hot_row{b}", [P, 8, P], BF16) for b in range(2)]
        hot_tile = [sb(f"hot_tile{b}", [P, 8, NJ], BF16) for b in range(2)]
        hot_value = [sb(f"hot_value{b}", [P, 8, 2 * NJ], BF16) for b in range(2)]
        zero_bf = sb("zero_bf", [P, 2 * NJ], BF16)
        rows_f = sb("rows_f", [P, NJ])
        rows_g = sb("rows_g", [P, NJ])
        rows_e = sb("rows_e", [P, NJ])
        to_rows = sb("to_rows", [P, NJ], U32)
        from_rows = sb("from_rows", [P, NJ], U32)
        ended = sb("ended", [1, NJ, E])
        tile_expert_f = sb("tile_expert_f", [1, NJ])
        tile_expert = sb("tile_expert", [1, NJ], I32)
        exps = sb("exps", [P, NTOK, E])
        exp2 = sb("exp2", [P, NTOK])
        gate = [sb(f"gate{c}", [P, NTOK]) for c in range(TOP)]
        gsum = sb("gsum", [P, NTOK])
        denom = sb("denom", [P, NTOK])

        RB = 4
        from_col = [sb(f"from_col{b}", [P, 1], U32) for b in range(RB)]
        to_col = [sb(f"to_col{b}", [P, 1], U32) for b in range(RB)]
        rows = [sb(f"rows{b}", [P, D]) for b in range(RB)]
        results = [sb(f"results{b}", [P, D]) for b in range(RB)]
        rowsT = [sb(f"rowsT{b}", [P, P]) for b in range(2)]
        hiddenT = tz[0:2]

        lane_bank = [psum(f"lane_bank{l}") for l in range(LANES)]
        bank_rz, bank_last, bank_hn, bank_xn = (psum(f"bank_{n}") for n in ("rz", "last", "hn", "xn"))

        bank_rows = lane_bank[2:4]
        bank_out = lane_bank[0:2]
        bank_hid = [bank_rz, bank_last]

        s_ident, s_const = sem("ident_set"), sem("const_set")
        s_wload, s_gload, s_wmoe, s_bload = sem("w_loaded"), sem("gru_w_loaded"), sem("moe_w_loaded"), sem("bias_loaded")
        s_wp, s_we = sem("w_product"), sem("w_evacuated")
        s_bcol = sem("bias_columns")
        s_bpart, s_bstore, s_brow, s_bzero = (sem("bias_part"), sem("bias_parts_stored"),
                                             sem("bias_rows_loaded"), sem("bias_rows_zeroed"))
        s_yzero = sem("y_zeroed")
        s_iota, s_iotaf = sem("iotas"), sem("iotas_float")
        s_route, s_mask, s_count = sem("routing_step"), sem("mask"), sem("counts")
        s_hot, s_hott, s_hotuse, s_table, s_texp = sem("one_hots"), sem("tile_one_hots"), sem("one_hots_used"), sem("table"), sem("tile_expert")
        s_shift, s_gexp = sem("logits_shifted"), sem("gate_exps")
        s_gate = sem("gates_step")
        s_go = sem("rows_may_move")
        s_fcol, s_tcol = sem("from_column"), sem("to_column")
        s_rows = [sem(f"rows_gathered{b}") for b in range(RB)]
        s_back = [sem(f"rows_scattered{b}") for b in range(RB)]
        s_xp, s_xe, s_w1, s_hp, s_ge, s_yp, s_ye = (
            sem(n) for n in ("rows_turned", "rows_turned_copied", "w1_copied", "hidden_product", "hidden_gelu",
                             "out_product", "out_copied"))
        s_yload = [sem(f"y_loaded{l}") for l in range(LANES)]
        s_first, s_both, s_out = sem("first_choice_added"), sem("both_added"), sem("out_stored")
        s_xload, s_cload = lane_sems("x_loaded"), lane_sems("ctx_loaded")
        s_fst_ = lane_sems("ln_stored")
        s_csq, s_cms, s_crms, s_cn, s_cT, s_cTe, s_kq, s_kqe, s_v, s_ve = (
            sem(n) for n in ("ctx_squares", "ctx_mean_square", "ctx_rms", "ctx_normed", "ctx_turned",
                                   "ctx_turned_copied", "kq_product", "kq_copied", "v_product", "v_copied"))
        s_xst, s_xmo, s_xve, s_xrs, s_xn_, s_xT = (
            sem(n) for n in ("x_stats", "x_moments", "x_variance", "x_rstd", "x_normed", "x_turned"))
        s_h0, s_h = sem("h_started"), sem("h_updated")
        s_sq, s_ssq, s_ms, s_rms, s_sc, s_scs, s_scT = (
            sem(n) for n in ("h_squares", "h_square_sum", "h_mean_square", "h_rms", "scores",
                                   "scores_scaled", "scores_turned"))
        s_pk, s_sub, s_exp, s_zs, s_zi, s_at = (
            sem(n) for n in ("peak", "scores_shifted", "exp", "exp_sum", "exp_inverse", "attn"))
        s_ase, s_ai, s_u, s_un, s_uT, s_uTe = (
            sem(n) for n in ("attn_sum_copied", "attn_inverse", "update_product",
                                   "update_normed", "update_turned", "update_copied"))
        s_R, s_HN, s_Z, s_XN, s_tr, s_hn, s_tz = (
            sem(n) for n in ("r_product", "hn_product", "z_product", "xn_product", "r_tanh", "hn_copied",
                                   "z_tanh"))
        s_rh, s_npre, s_n, s_hmn, s_zh = (
            sem(n) for n in ("r_times_hn", "n_sum", "n_tanh", "h_minus_n", "z_times"))
        s_hf, s_x2, s_fst, s_fmo, s_fve, s_frs, s_fln, s_fT, s_fTe, s_lg, s_lge, s_top, s_topi = (
            sem(n) for n in ("h_turned_back", "x2_ready", "x2_stats", "x2_moments", "x2_variance",
                                   "x2_rstd", "x2_normed", "ln_turned", "ln_turned_copied",
                                   "logits_product", "logits_copied", "top8_found", "top8_indexed"))

        def nth(l, n):
            return LANES * n + l + 1

        def wait_h(eng, l, n):
            if n % ITERS == 0:
                eng.wait_ge(s_h0, nth(l, n // ITERS))
            else:
                eng.wait_ge(s_h, nth(l, n - 1))

        ITER = ["score", "attend", "gates", "update"]
        CYCLE = len(ITER) * ITERS + 1
        LEAD_IN = 3
        SLOTS = LEAD_IN + CYCLE * ROUNDS + LANES

        def slots_of(r):
            start = LEAD_IN + CYCLE * r
            last = r == ROUNDS - 1
            yield "measure", 0, start - (7 if r else 3)
            yield "square", 0, start - 3
            yield "context", 0, start - (3 if r else 2)
            yield "norm", 0, start - 2
            yield "project", 0, start - (2 if r else 1)
            yield "begin", 0, start - (1 if r else 2)
            for i in range(ITERS):
                for k, stage in enumerate(ITER):
                    yield stage, ITERS * r + i, start + len(ITER) * i + k
            yield "finish", 0, start + CYCLE - 1
            yield "weigh", 0, start + CYCLE - 1 + (0 if last else 2)
            yield "route", 0, start + CYCLE - 1 + (1 if last else 7)
            yield "choose", 0, start + CYCLE - 1 + (1 if last else 8)

        plan = {}
        for l in range(LANES):
            for r in range(ROUNDS):
                for stage, n, at_ in slots_of(r):
                    assert (l + at_, stage) not in plan
                    plan[l + at_, stage] = (l, r, n)

        def at_slot(slot):
            return {stage: lrn for (t, stage), lrn in plan.items() if t == slot}

        def num(q, w):
            return q * RB + w

        def turn_of(q, w):
            return q + w // RB

        def wait_pos(eng, s, value):
            if not isinstance(value, int) or value > 0:
                eng.wait_ge(s, value)

        LEAD = 4

        def run_tiles(eng, step):
            last_q = (TILES - 1 - LEAD) // RB

            def plain(j):
                step(j // RB, j % RB, lambda k: 0 <= j + k < TILES)

            for j in range(RB):
                plain(j)
            with eng.Fori(1, last_q) as q:
                for w in range(RB):
                    step(q, w, lambda k: True)
            for j in range(RB * last_q, TILES + 1):
                plain(j)

        def group(t, g):
            return t[:, GB * g:GB * g + GB, :]

        def product_of(l, b):
            at = (D + 1) * (b % 3)
            return (lane_bank[l] if b < 3 else bank_last)[:, at:at + D + 1]

        block = stack.enter_context(nc.Block())

        @block.sync
        def _(sp):
            sp.dma_start(proj_in[:, :, :], proj).then_inc(s_wload, 16)
            sp.dma_start(col_in[:, :], columns).then_inc(s_wload, 16)
            sp.dma_start(group(x2, 0), x_g[0]).then_inc(s_xload[0], 16)
            sp.dma_start(c_in[0][:, :, :], ctx_g[0]).then_inc(s_cload[0], 16)
            sp.dma_start(gru_in[:, :, :, :], gru).then_inc(s_gload, 16)
            for l in range(1, LANES):
                sp.dma_start(group(x2, l), x_g[l]).then_inc(s_xload[l], 16)
                sp.dma_start(c_in[l][:, :, :], ctx_g[l]).then_inc(s_cload[l], 16)
            sp.dma_start(wg_sb[:, :], Wg).then_inc(s_wmoe, 16)
            sp.dma_start(w1_sb[:, :, 0:F], W1.rearrange("e d f -> d e f")).then_inc(s_wmoe, 16)
            sp.dma_start(w1_sb[:, :, F:], b1).then_inc(s_wmoe, 16)
            sp.dma_start(w2_sb[:, :, :, :], W2.rearrange("e (c p) d -> p e c d", p=P)).then_inc(s_wmoe, 16)
            sp.dma_start(b_in[:, :], b2.rearrange("e (q n) -> (e q) n", q=P // E)).then_inc(s_bload, 16)
            sp.wait_ge(s_bpart, 5)
            for k in range(3):
                sp.dma_start(bias_dram[k, :].rearrange("(p n) -> p n", p=P), b_parts[:, k, :]).then_inc(s_bstore, 16)
            sp.wait_ge(s_bstore, 48)
            sp.wait_ge(s_bzero, 1)
            sp.dma_start(b_rows[0:3, :], bias_dram).then_inc(s_brow, 16)
            sp.wait_ge(s_const, 1)
            ROWS_AT_ONCE = P * (2048 // D)
            for k in range(TOP * T // ROWS_AT_ONCE):
                sp.dma_start(y_dram[k * ROWS_AT_ONCE:(k + 1) * ROWS_AT_ONCE, :].rearrange("(p n) d -> p (n d)", p=P),
                             zeros[:, :]).then_inc(s_yzero, 16)
            for slot in range(SLOTS):
                now = at_slot(slot)
                if "route" in now:
                    l, r, _ = now["route"]
                    sp.wait_ge(s_fln, nth(l, r))
                    sp.dma_start(ln_g[LANES * r + l], work[l][:, :, :]).then_inc(s_fst_[l], 16)
                if "begin" in now:
                    l, r, _ = now["begin"]
                    if r + 1 < ROUNDS:
                        g = LANES * (r + 1) + l
                        sp.wait_ge(s_cn, nth(l, r))
                        sp.dma_start(c_in[l][:, :, :], ctx_g[g]).then_inc(s_cload[l], 16)
                        sp.wait_ge(s_xst, nth(l, r))
                        sp.dma_start(group(x2, g), x_g[g]).then_inc(s_xload[l], 16)

            for b in range(RB):
                sp.wait_ge(s_back[b], 16 * len(range(b, TILES, RB)))
            sp.wait_ge(s_yzero, 16 * (TOP * T // ROWS_AT_ONCE))
            y_c = y_dram.rearrange("(c k b s) d -> c k s b d", c=TOP, b=GB, s=P)
            out_g = out.rearrange("(g b) s d -> g s b d", b=GB)

            def load_results(k):
                if k >= LANES:
                    sp.wait_ge(s_both, k - LANES + 1)
                sp.dma_start(v[k % LANES][:, :, 0:D], y_c[0, k]).then_inc(s_yload[k % LANES], 16)
                sp.dma_start(c_in[k % LANES][:, :, :], y_c[1, k]).then_inc(s_yload[k % LANES], 16)

            for k in range(LANES):
                load_results(k)
            for k in range(NG):
                sp.wait_ge(s_both, k + 1)
                sp.dma_start(out_g[k], group(x2, k)).then_inc(s_out, 16)
                if k + LANES < NG:
                    load_results(k + LANES)
            sp.wait_ge(s_out, 16 * NG)

        @block.tensor
        def _(pe):
            pe.wait_ge(s_wload, 32)
            pe.matmul(bank_rz[:, 0:P], proj_in[:, 0, :], proj_in[:, 1, :], start=True, stop=True).then_inc(s_wp, 1)
            pe.wait_ge(s_ident, 2)

            def turn(bank, src):
                for b in range(GB):
                    last = pe.transpose(bank[:, b * P:(b + 1) * P], src[:, b, :], ident[:, :])
                return last

            def turn_context(l, r):
                pe.wait_ge(s_cn, nth(l, r))
                if r:
                    pe.wait_ge(s_uTe, nth(l, ITERS * r - 1))
                turn(lane_bank[l], work[l]).then_inc(s_cT, 1)

            def turn_x(l, r):
                pe.wait_ge(s_xn_, nth(l, r))
                if r:
                    pe.wait_ge(s_x2, nth(l, r - 1))
                    turn(lane_bank[l], work[l]).then_inc(s_xT, 1)
                else:
                    if l:
                        pe.wait_ge(s_h0, l)
                    turn(bank_hn, uT[l]).then_inc(s_xT, 1)

            def project_kq(l, r, _):
                pe.wait_ge(s_cTe, nth(l, r))
                pe.wait_ge(s_we, 3)
                pe.matmul(lane_bank[l][:, :], wkq[:, :], prob[l][:, :, :], start=True, stop=True)\
                    .then_inc(s_kq, 1)

            for slot in range(SLOTS):
                now = at_slot(slot)
                score, attend, gates = now.get("score"), now.get("attend"), now.get("gates")
                context, project, begin = now.get("context"), now.get("project"), now.get("begin")
                finish, route = now.get("finish"), now.get("route")
                if finish:
                    l, r, _ = finish
                    pe.wait_ge(s_h, nth(l, ITERS * r + ITERS - 1))
                    if r + 1 < ROUNDS:
                        pe.wait_ge(s_ve, nth(l, r + 1))
                    turn(lane_bank[l], hT[l]).then_inc(s_hf, 1)
                if project and not project[1]:
                    project_kq(*project)
                if gates:
                    l, _, n = gates
                    if l or n:
                        pe.wait_ge(s_tz, nth(l, n) - 1)
                    if n == 0:
                        pe.wait_ge(s_we, 4)
                        pe.wait_ge(s_h0, LANES)
                    wait_h(pe, l, n)
                    pe.matmul(bank_rz[:, :], whhT[:, 0, :], hT[l][:, :, :], start=True, stop=False)
                if score:
                    l, _, n = score
                    pe.wait_ge(s_sq, nth(l, n))
                    for b in range(GB):
                        last = pe.matmul(lane_bank[l][:, b:b + 1], work[l][:, b, :], ones_col[:, :],
                                         start=True, stop=True)
                    last.then_inc(s_ssq, 1)
                if begin and not begin[1]:
                    turn_x(*begin[0:2])
                if context and not context[1]:
                    turn_context(*context[0:2])
                if gates:
                    l, _, n = gates
                    pe.wait_ge(s_uTe, nth(l, n))
                    pe.matmul(bank_rz[:, :], wihT[:, 0, :], uT[l][:, :, :], start=False, stop=True)\
                        .then_inc(s_R, 1)
                if project and project[1]:
                    project_kq(*project)
                if score:
                    l, _, n = score
                    pe.wait_ge(s_ms, nth(l, n))
                    for b in range(GB):
                        last = pe.matmul(lane_bank[l][:, b * P:(b + 1) * P], hT[l][:, b, :], kq[l][:, b, :],
                                         start=True, stop=True)
                    last.then_inc(s_sc, 1)
                if attend:
                    l, _, n = attend
                    pe.wait_ge(s_at, nth(l, n))
                    if l or n:
                        pe.wait_ge(s_un, nth(l, n) - 1)
                    for b in range(GB):
                        last = pe.matmul(product_of(l, b), prob[l][:, b, :], v[l][:, b, :], start=True, stop=True)
                    last.then_inc(s_u, 1)
                if gates:
                    l, _, n = gates
                    if l or n:
                        pe.wait_ge(s_hn, nth(l, n) - 1)
                    pe.matmul(bank_hn[:, :], whhT[:, 2, :], hT[l][:, :, :], start=True, stop=True)\
                        .then_inc(s_HN, 1)
                if route:
                    l, r, _ = route
                    pe.wait_ge(s_fln, nth(l, r))
                    turn(lane_bank[l], work[l]).then_inc(s_fT, 1)
                if context and context[1]:
                    turn_context(*context[0:2])
                if project:
                    l, r, _ = project
                    pe.wait_ge(s_kqe, nth(l, r))
                    for b in range(GB):
                        last = pe.matmul(lane_bank[l][:, b * D:(b + 1) * D], prob[l][:, b, :], wvT[:, :],
                                         start=True, stop=True)
                    last.then_inc(s_v, 1)
                if begin and begin[1]:
                    turn_x(*begin[0:2])
                if score:
                    l, _, n = score
                    pe.wait_ge(s_scs, nth(l, n))
                    turn(lane_bank[l], work[l]).then_inc(s_scT, 1)
                if gates:
                    l, _, n = gates
                    pe.wait_ge(s_tr, nth(l, n))
                    pe.matmul(bank_rz[:, :], whhT[:, 1, :], hT[l][:, :, :], start=True, stop=False)
                if attend:
                    l, _, n = attend
                    pe.wait_ge(s_un, nth(l, n))
                    turn(lane_bank[l], work[l]).then_inc(s_uT, 1)
                if gates:
                    l, _, n = gates
                    pe.matmul(bank_rz[:, :], wihT[:, 1, :], uT[l][:, :, :], start=False, stop=True)\
                        .then_inc(s_Z, 1)
                if route:
                    l, r, _ = route
                    pe.wait_ge(s_fTe, nth(l, r))
                    pe.wait_ge(s_wmoe, 64)
                    for b in range(GB):
                        last = pe.matmul(lane_bank[l][:, b * E:(b + 1) * E], prob[l][:, b, :], wg_sb[:, :],
                                         start=True, stop=True)
                    last.then_inc(s_lg, 1)
                if gates:
                    l, _, n = gates
                    if l or n:
                        pe.wait_ge(s_npre, nth(l, n) - 1)
                    pe.matmul(bank_xn[:, :], wihT[:, 2, :], uT[l][:, :, :], start=True, stop=True)\
                        .then_inc(s_XN, 1)
            pe.wait_ge(s_const, 3)
            for c in range(TOP):
                pe.wait_ge(s_mask, c + 1)
                pe.matmul(bank_hid[c][:, 0:E * NTOK], before[:, :], mask[:, c], start=True, stop=True)
                pe.matmul(bank_hid[c][:, E * NTOK:2 * E * NTOK], ones_bf[:, :], mask[:, c],
                          start=True, stop=True).then_inc(s_count, 1)
            table = bank_hn[:, 0:2 * NJ]
            pe.wait_ge(s_iotaf, 5)
            pe.matmul(table, zero_bf[:, 0:P], zero_bf[:, :], start=True, stop=False).then_inc(s_hotuse, 2)
            with pe.Fori(0, NP // 16) as q:
                for b in range(2):
                    pe.wait_ge(s_hot, 2 * q + b + 1)
                    for i in range(8):
                        last = pe.matmul(table, hot_row[b][:, i, :], hot_value[b][:, i, :],
                                         start=False, stop=False)
                    last.then_inc(s_hotuse, 1)
            pe.matmul(table, zero_bf[:, 0:P], zero_bf[:, :], start=False, stop=True).then_inc(s_table, 1)

            pe.wait_ge(s_brow, 16)
            pe.wait_ge(s_texp, 1)

            def turn_rows(q, w):
                pe.wait_ge(s_rows[w % RB], 16 * (turn_of(q, w) + 1))
                wait_pos(pe, s_xe, num(q, w) - 1)
                pe.transpose(bank_rows[w % 2][:, 0:P], rows[w % RB][:, :], ident[:, :]).then_inc(s_xp, 1)

            def first_layer(q, w):
                pe.wait_ge(s_w1, num(q, w) + 1)
                pe.wait_ge(s_xe, num(q, w) + 1)
                wait_pos(pe, s_ge, num(q, w) - 1)
                for c in range(FC):
                    last = pe.matmul(bank_hid[w % 2][:, c * P:(c + 1) * P], w1_now[w % 2][:, c * P:(c + 1) * P],
                                     rowsT[w % 2][:, :], start=True, stop=True)
                last.then_inc(s_hp, 1)

            def second_layer(q, w):
                e = pe.value_load(tile_expert[0:1, bass.ds(num(q, w), 1)], min_val=0, max_val=E - 1)
                pe.wait_ge(s_ge, num(q, w) + 1)
                wait_pos(pe, s_ye, num(q, w) - 1)
                pe.matmul(bank_out[w % 2][:, 0:D], ones_bf[:, :], b_rows[:, bass.ds(e * D, D)],
                          start=True, stop=False)
                for c in range(FC):
                    last = pe.matmul(bank_out[w % 2][:, 0:D], hiddenT[w % 2][:, c, :],
                                     w2_flat[:, bass.ds(e * F + c * D, D)], start=False, stop=(c == FC - 1))
                last.then_inc(s_yp, 1)

            turn_rows(0, 0)
            turn_rows(0, 1)
            first_layer(0, 0)

            def pe_step(q, w, has):
                if has(1):
                    first_layer(q, w + 1)
                if has(2):
                    turn_rows(q, w + 2)
                if has(0):
                    second_layer(q, w)

            run_tiles(pe, pe_step)

        @block.scalar
        def _(act):
            def copy_context(l, r):
                act.wait_ge(s_cT, nth(l, r))
                act.activation(prob[l][:, :, :], lane_bank[l][:, :], ACT.Copy).then_inc(s_cTe, 1)

            def copy_x(l, r):
                act.wait_ge(s_xT, nth(l, r))
                act.activation(hT[l][:, :, :], (lane_bank[l] if r else bank_hn)[:, :], ACT.Copy).then_inc(s_h0, 1)

            def copy_kq(l, r, _):
                act.wait_ge(s_kq, nth(l, r))
                act.wait_ge(s_bcol, 3)
                act.activation(kq[l][:, :, :], lane_bank[l][:, :], ACT.Copy, scale=slot_scale[:, :])\
                    .then_inc(s_kqe, 1)

            for slot in range(SLOTS):
                now = at_slot(slot)
                score, attend, gates, update = (now.get(k) for k in ITER)
                context, project, begin = now.get("context"), now.get("project"), now.get("begin")
                square, route = now.get("square"), now.get("route")
                if score:
                    l, r, n = score
                    wait_h(act, l, n)
                    if r and n == ITERS * r + 2:
                        act.wait_ge(s_fst_[l], 16 * r)
                    act.activation(work[l][:, :, :], hT[l][:, :, :], ACT.Square).then_inc(s_sq, 1)
                if square:
                    l, r, _ = square
                    act.wait_ge(s_cload[l], 16 * (r + 1))
                    for b in range(GB):
                        last = act.activation(prob[l][:, b, :], c_in[l][:, b, :], ACT.Square,
                                              accum_out=csum[l][:, b:b + 1])
                    last.then_inc(s_csq, 1)
                if project and not project[1]:
                    copy_kq(*project)
                if begin and not begin[1]:
                    copy_x(*begin[0:2])
                if context and not context[1]:
                    copy_context(*context[0:2])
                if update:
                    l, _, n = update
                    act.wait_ge(s_npre, nth(l, n))
                    act.activation(tr[l][:, :, :], tr[l][:, :, :], ACT.Tanh, bias=col_in[:, 2:3])\
                        .then_inc(s_n, 1)
                if project and project[1]:
                    copy_kq(*project)
                if gates:
                    l, _, n = gates
                    act.wait_ge(s_R, nth(l, n))
                    if n == 0:
                        act.wait_ge(s_bcol, 3)
                    act.activation(tr[l][:, :, :], bank_rz[:, :], ACT.Tanh, bias=bias_rz[:, 0:1], scale=0.5)\
                        .then_inc(s_tr, 1)
                    act.wait_ge(s_HN, nth(l, n))
                    act.activation(hn[l][:, :, :], bank_hn[:, :], ACT.Identity, bias=bias_hn[:, :])\
                        .then_inc(s_hn, 1)
                if context and context[1]:
                    copy_context(*context[0:2])
                if begin and begin[1]:
                    copy_x(*begin[0:2])
                if project:
                    l, r, _ = project
                    act.wait_ge(s_v, nth(l, r))
                    act.activation(v[l][:, :, 0:D], lane_bank[l][:, :].rearrange("p (b d) -> p b d", b=GB), ACT.Copy)\
                        .then_inc(s_ve, 1)
                if route:
                    l, r, _ = route
                    act.wait_ge(s_fT, nth(l, r))
                    act.activation(prob[l][:, :, :], lane_bank[l][:, :], ACT.Copy).then_inc(s_fTe, 1)
                if attend:
                    l, _, n = attend
                    act.wait_ge(s_uT, nth(l, n))
                    act.activation(uT[l][:, :, :], lane_bank[l][:, :], ACT.Copy).then_inc(s_uTe, 1)
                if score:
                    l, _, n = score
                    act.wait_ge(s_sub, nth(l, n))
                    act.activation(prob[l][:, :, :], prob[l][:, :, :], ACT.Exp).then_inc(s_exp, 1)
                if gates:
                    l, _, n = gates
                    act.wait_ge(s_Z, nth(l, n))
                    act.activation(tz[l][:, :, :], bank_rz[:, :], ACT.Tanh, bias=bias_rz[:, 1:2], scale=0.5)\
                        .then_inc(s_tz, 1)
            act.wait_ge(s_shift, 2)
            act.activation(exps[:, :, :], exps[:, :, :], ACT.Exp).then_inc(s_gexp, 1)
            act.activation(exp2[:, :], exp2[:, :], ACT.Exp).then_inc(s_gexp, 1)

            def copy_rows(q, w):
                act.wait_ge(s_xp, num(q, w) + 1)
                wait_pos(act, s_hp, num(q, w) - 1)
                act.activation(rowsT[w % 2][:, :], bank_rows[w % 2][:, 0:P], ACT.Copy).then_inc(s_xe, 1)

            def gelu(q, w):
                act.wait_ge(s_hp, num(q, w) + 1)
                wait_pos(act, s_yp, num(q, w) - 1)
                for c in range(FC):
                    last = act.activation(hiddenT[w % 2][:, c, :], bank_hid[w % 2][:, c * P:(c + 1) * P], ACT.Gelu,
                                          bias=w1_now[w % 2][:, F + c:F + c + 1])
                last.then_inc(s_ge, 1)

            copy_rows(0, 0)
            copy_rows(0, 1)

            def act_step(q, w, has):
                if has(0):
                    gelu(q, w)
                if has(2):
                    copy_rows(q, w + 2)

            run_tiles(act, act_step)

        @block.vector
        def _(dve):
            def spread(column):
                return column[:, :].unsqueeze(2).to_broadcast([P, GB, P])

            def bank3(bank):
                return bank[:, :].rearrange("p (b s) -> p b s", b=GB)

            def first3(l):
                return lane_bank[l][:, 0:3 * (D + 1)].rearrange("p (b d) -> p b d", b=3)

            dve.wait_ge(s_wload, 32)
            dve.tensor_tensor(bias_rz[:, :], col_in[:, 0:2], col_in[:, 3:5], ALU.add).then_inc(s_we, 1)
            dve.wait_ge(s_we, 1)
            dve.tensor_scalar(bias_rz[:, :], bias_rz[:, :], 0.5, None, ALU.mult).then_inc(s_bcol, 1)
            dve.tensor_scalar(bias_hn[:, :], col_in[:, 5:6], 0.5, None, ALU.mult).then_inc(s_bcol, 1)
            dve.tensor_scalar(slot_scale[:, :], col_in[:, 6:7], SCALE, None, ALU.mult).then_inc(s_bcol, 1)
            dve.tensor_scalar(wvT[:, :], proj_in[:, 2, :], col_in[:, 7:8], None, ALU.mult).then_inc(s_we, 1)
            dve.wait_ge(s_wp, 1)
            dve.tensor_scalar(wkq[:, :], bank_rz[:, 0:P], col_in[:, 7:8], None, ALU.mult).then_inc(s_we, 1)
            dve.wait_ge(s_gload, 16)
            dve.tensor_scalar(whhT[:, 2, :], whhT[:, 2, :], 0.5, None, ALU.mult).then_inc(s_we, 1)

            def bias_parts():
                dve.wait_ge(s_bload, 16)
                dve.tensor_copy(b_parts[:, 0, :], b_in[:, :]).then_inc(s_bpart, 1)
                dve.wait_ge(s_bpart, 1)
                dve.tensor_tensor(b_rest[:, 0, :], b_in[:, :], b_parts[:, 0, :], ALU.subtract).then_inc(s_bpart, 1)
                dve.wait_ge(s_bpart, 2)
                dve.tensor_copy(b_parts[:, 1, :], b_rest[:, 0, :]).then_inc(s_bpart, 1)
                dve.wait_ge(s_bpart, 3)
                dve.tensor_tensor(b_rest[:, 1, :], b_rest[:, 0, :], b_parts[:, 1, :], ALU.subtract)\
                    .then_inc(s_bpart, 1)
                dve.wait_ge(s_bpart, 4)
                dve.tensor_copy(b_parts[:, 2, :], b_rest[:, 1, :]).then_inc(s_bpart, 1)

            def moments_of(g, l, times, st, mo, ve):
                for b in range(GB):
                    last = dve.bn_stats(stats[l][:, b, :], x2[:, GB * g + b, :])
                last.then_inc(st, 1)
                dve.wait_ge(st, times)
                for b in range(GB):
                    last = dve.bn_aggr(moments[l][:, b, :], stats[l][:, b, :])
                last.then_inc(mo, 1)
                dve.wait_ge(mo, times)
                dve.tensor_scalar(rstd[l][:, :], moments[l][:, :, 1], 1e-5, None, ALU.add).then_inc(ve, 1)

            def normed(g, l, to, done):
                for b in range(GB):
                    last = dve.tensor_scalar(to[:, b, :], x2[:, GB * g + b, :], moments[l][:, b, 0:1],
                                             rstd[l][:, b:b + 1], ALU.subtract, ALU.mult)
                last.then_inc(done, 1)

            def norm_x2(l, r, _):
                dve.wait_ge(s_frs, nth(l, r))
                dve.wait_ge(s_uT, nth(l, ITERS * (r + 1) + (-1 if r + 1 == ROUNDS else 1)))
                normed(LANES * r + l, l, work[l], s_fln)

            def mean_square(l, r, _):
                dve.wait_ge(s_csq, nth(l, r))
                dve.tensor_scalar(crms[l][:, :], csum[l][:, :], 1.0 / D, 1e-6, ALU.mult, ALU.add)\
                    .then_inc(s_cms, 1)

            def measure_x(l, r, _):
                dve.wait_ge(s_xload[l], 16 * (r + 1))
                moments_of(LANES * r + l, l, nth(l, r), s_xst, s_xmo, s_xve)

            def norm_x(l, r, _):
                dve.wait_ge(s_xrs, nth(l, r))
                if r:
                    dve.wait_ge(s_cT, nth(l, r))
                normed(LANES * r + l, l, work[l] if r else uT[l], s_xn_)

            def choose_experts(l, r, _):
                g = LANES * r + l
                dve.wait_ge(s_lg, nth(l, r))
                dve.tensor_copy(group(logits, g),
                                lane_bank[l][:, 0:GB * E].rearrange("p (b e) -> p b e", b=GB))\
                    .then_inc(s_lge, 1)
                dve.wait_ge(s_lge, nth(l, r))
                for b in range(GB):
                    last = dve.max(top8[:, GB * g + b, :], logits[:, GB * g + b, :])
                last.then_inc(s_top, 1)
                dve.wait_ge(s_top, nth(l, r))
                for b in range(GB):
                    last = dve.max_index(top8_at[:, GB * g + b, :], top8[:, GB * g + b, :],
                                         logits[:, GB * g + b, :])
                last.then_inc(s_topi, 1)

            for slot in range(SLOTS):
                now = at_slot(slot)
                score, attend, update = now.get("score"), now.get("attend"), now.get("update")
                measure, square, context = now.get("measure"), now.get("square"), now.get("context")
                norm, finish, weigh = now.get("norm"), now.get("finish"), now.get("weigh")
                route, choose = now.get("route"), now.get("choose")
                if slot == 6:
                    bias_parts()
                if square and square[1]:
                    mean_square(*square)
                if attend:
                    l, _, n = attend
                    dve.wait_ge(s_exp, nth(l, n))
                    dve.tensor_reduce(zsum[l][:, :], prob[l][:, :, :], AX.X, ALU.add).then_inc(s_zs, 1)
                    dve.wait_ge(s_zs, nth(l, n))
                    dve.reciprocal(zinv[l][:, :], zsum[l][:, :]).then_inc(s_zi, 1)
                if finish:
                    l, r, _ = finish
                    xg = group(x2, LANES * r + l)
                    dve.wait_ge(s_hf, nth(l, r))
                    dve.tensor_tensor(xg, bank3(lane_bank[l]), xg, ALU.add).then_inc(s_x2, 1)
                if update:
                    l, _, n = update
                    dve.wait_ge(s_tr, nth(l, n))
                    dve.wait_ge(s_hn, nth(l, n))
                    dve.scalar_tensor_tensor(tr[l][:, :, :], tr[l][:, :, :], 1.0, hn[l][:, :, :],
                                             ALU.add, ALU.mult).then_inc(s_rh, 1)
                if score:
                    l, _, n = score
                    dve.wait_ge(s_ssq, nth(l, n))
                    dve.tensor_scalar(rms[l][:, :], lane_bank[l][:, 0:GB], 1.0 / D, 1e-6, ALU.mult, ALU.add)\
                        .then_inc(s_ms, 1)
                if update:
                    l, _, n = update
                    dve.wait_ge(s_rh, nth(l, n))
                    dve.wait_ge(s_XN, nth(l, n))
                    dve.tensor_tensor(tr[l][:, :, :], tr[l][:, :, :], bank3(bank_xn), ALU.add)\
                        .then_inc(s_npre, 1)
                if context:
                    l, r, _ = context
                    dve.wait_ge(s_crms, nth(l, r))
                    dve.tensor_tensor(work[l][:, :, :], c_in[l][:, :, :], spread(crms[l]), ALU.mult)\
                        .then_inc(s_cn, 1)
                if norm and not norm[1]:
                    norm_x(*norm)
                if measure:
                    measure_x(*measure)
                if square and not square[1]:
                    mean_square(*square)
                if choose and choose[1] + 1 < ROUNDS:
                    choose_experts(*choose)
                if route:
                    norm_x2(*route)
                if weigh:
                    l, r, _ = weigh
                    dve.wait_ge(s_x2, nth(l, r))
                    moments_of(LANES * r + l, l, nth(l, r), s_fst, s_fmo, s_fve)
                if score:
                    l, _, n = score
                    dve.wait_ge(s_sc, nth(l, n))
                    dve.wait_ge(s_rms, nth(l, n))
                    dve.tensor_tensor(work[l][:, :, :], bank3(lane_bank[l]), spread(rms[l]), ALU.mult)\
                        .then_inc(s_scs, 1)
                if attend:
                    l, _, n = attend
                    dve.wait_ge(s_u, nth(l, n))
                    dve.tensor_scalar(asum[l][:, 0:3], first3(l)[:, :, D], 1e-6, None, ALU.add)
                    dve.tensor_scalar(asum[l][:, 3:4], product_of(l, 3)[:, D:D + 1], 1e-6, None, ALU.add)\
                        .then_inc(s_ase, 1)
                    dve.wait_ge(s_ase, nth(l, n))
                    dve.reciprocal(ainv[l][:, :], asum[l][:, :]).then_inc(s_ai, 1)
                    dve.wait_ge(s_ai, nth(l, n))
                    dve.tensor_tensor(work[l][:, 0:3, :], first3(l)[:, :, 0:D],
                                      ainv[l][:, 0:3].unsqueeze(2).to_broadcast([P, 3, D]), ALU.mult)
                    dve.tensor_scalar(work[l][:, 3, :], product_of(l, 3)[:, 0:D], ainv[l][:, 3:4], None, ALU.mult)\
                        .then_inc(s_un, 1)
                if score:
                    l, _, n = score
                    dve.wait_ge(s_scT, nth(l, n))
                    dve.tensor_reduce(peak[l][:, :], bank3(lane_bank[l]), AX.X, ALU.max).then_inc(s_pk, 1)
                    dve.wait_ge(s_pk, nth(l, n))
                    dve.tensor_tensor(prob[l][:, :, :], bank3(lane_bank[l]), spread(peak[l]), ALU.subtract)\
                        .then_inc(s_sub, 1)
                if update:
                    l, _, n = update
                    dve.wait_ge(s_hmn, nth(l, n))
                    dve.wait_ge(s_tz, nth(l, n))
                    dve.scalar_tensor_tensor(hn[l][:, :, :], tz[l][:, :, :], 1.0, hn[l][:, :, :],
                                             ALU.add, ALU.mult).then_inc(s_zh, 1)
                    dve.wait_ge(s_zh, nth(l, n))
                    dve.scalar_tensor_tensor(hT[l][:, :, :], hn[l][:, :, :], 0.5, tr[l][:, :, :],
                                             ALU.mult, ALU.add).then_inc(s_h, 1)
                if norm and norm[1]:
                    norm_x(*norm)
                if choose and choose[1] + 1 == ROUNDS:
                    choose_experts(*choose)

            steps = [0]

            def link(ins):
                steps[0] += 1
                ins.then_inc(s_route, 1)
                dve.wait_ge(s_route, steps[0])

            def per_token(t):
                return t.unsqueeze(1).to_broadcast([P, E, NTOK])

            def per_expert(t):
                return t.unsqueeze(2).to_broadcast([P, E, NTOK])

            dve.wait_ge(s_topi, NG)
            dve.wait_ge(s_iotaf, 5)
            for c in range(TOP):
                link(dve.tensor_copy(at[:, c, :], top8_at[:, :, c]))
            for c in range(TOP):
                dve.tensor_tensor(mask[:, c], per_token(at[:, c, :]), per_expert(iota_f[:, 0:E]), ALU.is_equal)\
                    .then_inc(s_mask, 1)
            dve.tensor_tensor(exps[:, :, :], logits[:, :, :], top8[:, :, 0:1].to_broadcast([P, NTOK, E]),
                              ALU.subtract).then_inc(s_shift, 1)
            dve.tensor_tensor(exp2[:, :], top8[:, :, 1], top8[:, :, 0], ALU.subtract).then_inc(s_shift, 1)
            dve.wait_ge(s_mask, 2)
            for c in range(TOP):
                in_tile_count = bank_hid[c][:, 0:E * NTOK].rearrange("p (e t) -> p e t", e=E)
                total = bank_hid[c][:, E * NTOK:2 * E * NTOK]
                flat = upto[:, c].rearrange("p e t -> p (e t)")
                dve.wait_ge(s_count, c + 1)
                link(dve.tensor_tensor_scan(flat, restart[:, :, :].rearrange("p e t -> p (e t)"), total, 0.0,
                                            ALU.mult, ALU.add))
                link(dve.tensor_tensor(place[:, c], upto[:, c], total.rearrange("p (e t) -> p e t", e=E),
                                       ALU.subtract))
                link(dve.tensor_tensor(place[:, c], place[:, c], in_tile_count, ALU.add))
                if c:
                    link(dve.tensor_tensor(place[:, c], place[:, c], per_expert(upto[:, 0, :, NTOK - 1]), ALU.add))
                link(dve.tensor_tensor(place[:, c], place[:, c], mask[:, c], ALU.mult))
                link(dve.tensor_reduce(pos[:, c, :], place[:, c].rearrange("p e t -> p t e"), AX.X, ALU.add))
            link(dve.tensor_scalar(keep[:, :, :], pos[:, :, :], float(CAP), None, ALU.is_lt))
            link(dve.tensor_scalar(pos[:, :, :], pos[:, :, :], float(CAP - 1), None, ALU.min))
            link(dve.tensor_tensor(filled[:, :], upto[:, 0, :, NTOK - 1], upto[:, 1, :, NTOK - 1], ALU.add))
            link(dve.tensor_scalar(filled[:, :], filled[:, :], float(CAP), None, ALU.min))
            link(dve.tensor_tensor(compare[:, 0:E, :], filled[:, :].unsqueeze(2).to_broadcast([P, E, QS]),
                                   steps128[:, :].unsqueeze(1).to_broadcast([P, E, QS]), ALU.is_gt))
            link(dve.tensor_reduce(tiles_of[:, :], compare[:, 0:E, :], AX.X, ALU.add))
            link(dve.tensor_tensor_scan(tile_end[:, :], restart[:, 0, 1:1 + E], tiles_of[:, :], 0.0,
                                        ALU.mult, ALU.add))
            link(dve.tensor_tensor(tile_base[:, :], tile_end[:, :], tiles_of[:, :], ALU.subtract))
            for c in range(TOP):
                link(dve.tensor_tensor(place[:, c], mask[:, c], per_expert(tile_base[:, :]), ALU.mult))
                link(dve.tensor_reduce(base_of[:, c, :], place[:, c].rearrange("p e t -> p t e"), AX.X, ALU.add))
            pos_f = pos[:, :, :].rearrange("p c t -> p (c t)")
            depth_f = depth[:, :, :].rearrange("p c t -> p (c t)")
            link(dve.tensor_tensor(compare[:, :, :], pos_f.unsqueeze(2).to_broadcast([P, NP, QS]),
                                   steps128[:, :].unsqueeze(1).to_broadcast([P, NP, QS]), ALU.is_ge))
            link(dve.tensor_reduce(depth_f, compare[:, :, :], AX.X, ALU.add))
            link(dve.scalar_tensor_tensor(in_tile[:, :], depth_f, -float(P), pos_f, ALU.mult, ALU.add))
            link(dve.tensor_scalar(in_tile[:, :], in_tile[:, :], float(P), None, ALU.add))
            link(dve.tensor_tensor(which[:, :], depth_f, base_of[:, :, :].rearrange("p c t -> p (c t)"), ALU.add))
            link(dve.tensor_scalar(pos[:, :, :], keep[:, :, :], -1000.0, 999.0, ALU.mult, ALU.add))
            link(dve.tensor_tensor(which[:, :], which[:, :], pos_f, ALU.add))
            with dve.Fori(0, NP // 16) as q:
                for b in range(2):
                    pairs = bass.ds(16 * q + 8 * b, 8)
                    dve.wait_ge(s_hotuse, 2 * q + b + 1)
                    dve.tensor_tensor(hot_row[b][:, :, :], in_tile[:, pairs].unsqueeze(2).to_broadcast([P, 8, P]),
                                      iota_f[:, :].unsqueeze(1).to_broadcast([P, 8, P]), ALU.is_equal)
                    dve.tensor_tensor(hot_tile[b][:, :, :], which[:, pairs].unsqueeze(2).to_broadcast([P, 8, NJ]),
                                      iota_f[:, 0:NJ].unsqueeze(1).to_broadcast([P, 8, NJ]), ALU.is_equal)\
                        .then_inc(s_hott, 1)
                    dve.wait_ge(s_hott, 2 * q + b + 1)
                    dve.tensor_tensor(hot_value[b][:, :, 0:NJ], hot_tile[b][:, :, :],
                                      iota_f[:, bass.ds(16 * q + 8 * b + 1, 8)].unsqueeze(2)
                                      .to_broadcast([P, 8, NJ]), ALU.mult)
                    dve.tensor_scalar(hot_value[b][:, :, NJ:2 * NJ], hot_tile[b][:, :, :], row_f[:, :], None,
                                      ALU.mult).then_inc(s_hot, 1)
            dve.tensor_tensor(ended[:, :, :], tile_end[0:1, :].unsqueeze(1).to_broadcast([1, NJ, E]),
                              iota_f[0:1, 0:NJ].unsqueeze(2).to_broadcast([1, NJ, E]), ALU.is_le)\
                .then_inc(s_gate, 1)
            dve.wait_ge(s_gate, 1)
            dve.tensor_reduce(tile_expert_f[:, :], ended[:, :, :], AX.X, ALU.add).then_inc(s_gate, 1)
            dve.wait_ge(s_gate, 2)
            dve.tensor_scalar(tile_expert[:, :], tile_expert_f[:, :], float(E - 1), None, ALU.min)\
                .then_inc(s_texp, 1)
            table_tile, table_row = bank_hn[:, 0:NJ], bank_hn[:, NJ:2 * NJ]
            dve.wait_ge(s_table, 1)
            link(dve.tensor_scalar(rows_f[:, :], table_tile, float(P), -float(P), ALU.mult, ALU.add))
            link(dve.tensor_tensor(rows_f[:, :], rows_f[:, :], table_row, ALU.add))
            link(dve.tensor_scalar(rows_g[:, :], rows_f[:, :], float(T), -float(T), ALU.is_ge, ALU.mult))
            link(dve.tensor_tensor(rows_g[:, :], rows_g[:, :], rows_f[:, :], ALU.add))
            link(dve.tensor_scalar(from_rows[:, :], rows_g[:, :], 0.0, None, ALU.max))
            link(dve.tensor_scalar(rows_e[:, :], table_tile, 0.0, INVALID, ALU.is_equal, ALU.mult))
            link(dve.tensor_tensor(to_rows[:, :], rows_f[:, :], rows_e[:, :], ALU.add))

            def from_column(q, w):
                if not (isinstance(q, int) and turn_of(q, w) == 0):
                    dve.wait_ge(s_rows[w % RB], 16 * turn_of(q, w))
                dve.tensor_copy(from_col[w % RB][:, :], from_rows[:, bass.ds(num(q, w), 1)]).then_inc(s_fcol, 1)

            def to_column(q, w):
                if not (isinstance(q, int) and turn_of(q, w) == 0):
                    dve.wait_ge(s_back[w % RB], 16 * turn_of(q, w))
                dve.tensor_copy(to_col[w % RB][:, :], to_rows[:, bass.ds(num(q, w), 1)]).then_inc(s_tcol, 1)

            def copy_w1(q, w):
                e = dve.value_load(tile_expert[0:1, bass.ds(num(q, w), 1)], min_val=0, max_val=E - 1)
                wait_pos(dve, s_ge, num(q, w) - 1)
                wait_pos(dve, s_hp, num(q, w) - 1)
                dve.tensor_copy(w1_now[w % 2][:, :], w1_flat[:, bass.ds(e * (F + FC), F + FC)]).then_inc(s_w1, 1)

            def copy_results(q, w):
                dve.wait_ge(s_yp, num(q, w) + 1)
                dve.tensor_copy(results[w % RB][:, :], bank_out[w % 2][:, 0:D]).then_inc(s_ye, 1)

            for j in range(LEAD):
                from_column(0, j)
            dve.wait_ge(s_texp, 1)
            for j in range(2):
                copy_w1(0, j)
            dve.wait_ge(s_gexp, 2)
            gsteps = [2]

            def glink(ins):
                gsteps[0] += 1
                ins.then_inc(s_gate, 1)
                dve.wait_ge(s_gate, gsteps[0])

            glink(dve.tensor_reduce(gsum[:, :], exps[:, :, :], AX.X, ALU.add))
            glink(dve.reciprocal(gate[0][:, :], gsum[:, :]))
            glink(dve.tensor_tensor(gate[1][:, :], gate[0][:, :], exp2[:, :], ALU.mult))
            glink(dve.scalar_tensor_tensor(denom[:, :], gate[0][:, :], 1e-9, gate[1][:, :], ALU.add, ALU.add))
            glink(dve.reciprocal(gsum[:, :], denom[:, :]))
            for c in range(TOP):
                glink(dve.tensor_tensor(gate[c][:, :], gate[c][:, :], gsum[:, :], ALU.mult))
                glink(dve.tensor_tensor(gate[c][:, :], gate[c][:, :], keep[:, c, :], ALU.mult))

            def dve_step(q, w, has):
                if has(LEAD):
                    from_column(q, w + LEAD)
                if has(2):
                    copy_w1(q, w + 2)
                if has(0):
                    to_column(q, w)
                    copy_results(q, w)

            run_tiles(dve, dve_step)

            for k in range(NG):
                dve.wait_ge(s_yload[k % LANES], 32 * (k // LANES + 1))
                for c, y in enumerate((v[k % LANES], c_in[k % LANES])):
                    if c:
                        dve.wait_ge(s_first, k + 1)
                    for b in range(GB):
                        t = GB * k + b
                        last = dve.scalar_tensor_tensor(x2[:, t, :], y[:, b, 0:D], gate[c][:, t:t + 1], x2[:, t, :],
                                                        ALU.mult, ALU.add)
                    last.then_inc(s_both if c else s_first, 1)

        @block.gpsimd
        def _(pool):
            pool.memset(ident[:, :], 0.0).then_inc(s_ident, 1)
            pool.memset(ones_col[:, :], 1.0)
            pool.memset(neg_half[:, :], -0.5)
            for l in range(LANES):
                pool.memset(v[l][:, :, D:], 1.0)
            pool.wait_ge(s_ident, 1)
            pool.affine_select(out=ident[:, :], in_=ident[:, :], compare_op=ALU.not_equal, fill=1.0, base=0,
                               pattern=[[-1, P]], channel_multiplier=1).then_inc(s_ident, 1)
            pool.memset(zeros[:, :], 0.0).then_inc(s_const, 1)
            pool.memset(b_rows[:, :], 0.0).then_inc(s_bzero, 1)
            pool.memset(ones_bf[:, :], 1.0).then_inc(s_const, 1)
            pool.wait_ge(s_const, 2)
            pool.affine_select(out=before[:, :], in_=ones_bf[:, :], compare_op=ALU.is_gt, fill=0.0, base=0,
                               pattern=[[1, P]], channel_multiplier=-1).then_inc(s_const, 1)
            pool.iota(iota_i[:, :], [[1, P]], base=0, channel_multiplier=0).then_inc(s_iota, 1)
            pool.iota(row_i[:, :], [[1, 1]], base=0, channel_multiplier=1).then_inc(s_iota, 1)
            pool.memset(restart[:, :, :], 1.0).then_inc(s_iota, 1)
            pool.memset(zero_bf[:, :], 0.0).then_inc(s_iotaf, 1)
            pool.wait_ge(s_iota, 3)
            pool.tensor_copy(iota_f[:, :], iota_i[:, :]).then_inc(s_iotaf, 1)
            pool.tensor_copy(row_f[:, :], row_i[:, :]).then_inc(s_iotaf, 1)
            pool.memset(restart[:, :, 0:1], 0.0).then_inc(s_iotaf, 1)
            pool.wait_ge(s_iotaf, 4)
            pool.tensor_scalar(steps128[:, :], iota_f[:, 0:QS], float(P), None, ALU.mult).then_inc(s_iotaf, 1)
            def inverse_root(column, ready, done, times):
                pool.wait_ge(ready, times)
                pool.tensor_tensor(column[:, :], column[:, :], neg_half[:, :], ALU.pow).then_inc(done, 1)

            for slot in range(SLOTS):
                now = at_slot(slot)
                if "square" in now and now["square"][1]:
                    l, r, _ = now["square"]
                    inverse_root(crms[l], s_cms, s_crms, nth(l, r))
                if "attend" in now:
                    l, _, n = now["attend"]
                    pool.wait_ge(s_zi, nth(l, n))
                    pool.tensor_tensor(prob[l][:, :, :], prob[l][:, :, :],
                                       zinv[l][:, :].unsqueeze(2).to_broadcast([P, GB, P]), ALU.mult)\
                        .then_inc(s_at, 1)
                if "score" in now:
                    l, _, n = now["score"]
                    inverse_root(rms[l], s_ms, s_rms, nth(l, n))
                if "measure" in now:
                    l, r, _ = now["measure"]
                    inverse_root(rstd[l], s_xve, s_xrs, nth(l, r))
                if "square" in now and not now["square"][1]:
                    l, r, _ = now["square"]
                    inverse_root(crms[l], s_cms, s_crms, nth(l, r))
                if "update" in now:
                    l, _, n = now["update"]
                    pool.wait_ge(s_n, nth(l, n))
                    pool.tensor_tensor(hn[l][:, :, :], hT[l][:, :, :], tr[l][:, :, :], ALU.subtract)\
                        .then_inc(s_hmn, 1)

                if "weigh" in now:
                    l, r, _ = now["weigh"]
                    inverse_root(rstd[l], s_fve, s_frs, nth(l, r))
            for l in range(LANES):
                pool.wait_ge(s_fst_[l], 16 * ROUNDS)
            pool.wait_ge(s_yzero, 16 * (TOP * T // (P * (2048 // D))))

            def gather(q, w):
                pool.wait_ge(s_fcol, num(q, w) + 1)
                wait_pos(pool, s_xp, num(q, w) - RB + 1)
                pool.sem_inc(s_go, 1)
                pool.indirect_dma_start(rows[w % RB][:, :], None, ln_dram,
                                        bass.IndirectOffsetOnAxis(ap=from_col[w % RB][:, 0:1], axis=0))\
                    .then_inc(s_rows[w % RB], 16)

            def scatter(q, w):
                pool.wait_ge(s_tcol, num(q, w) + 1)
                pool.wait_ge(s_ye, num(q, w) + 1)
                pool.sem_inc(s_go, 1)
                pool.indirect_dma_start(y_dram, bass.IndirectOffsetOnAxis(ap=to_col[w % RB][:, 0:1], axis=0),
                                        results[w % RB][:, :], None, bounds_check=TOP * T - 1, oob_is_err=False)\
                    .then_inc(s_back[w % RB], 16)

            for j in range(LEAD):
                gather(0, j)

            def pool_step(q, w, has):
                if has(LEAD):
                    gather(q, w + LEAD)
                if has(0):
                    scatter(q, w)

            run_tiles(pool, pool_step)



def kernel(**inputs):
    import numpy as _np
    import concourse.bacc as _bacc
    from concourse import mybir as _mybir
    from concourse.bass_utils import run_bass_kernel_spmd as _run

    nc = _bacc.Bacc("TRN2", target_bir_lowering=False, num_devices=1)
    arrays, args = {}, []
    w = {k.removeprefix("L0_").removeprefix("xattn_").removeprefix("ffn_"): _np.asarray(a) for k, a in inputs.items()}
    D = w["Wq"].shape[0]

    def turned(m):
        return m.reshape(3, D, D).transpose(2, 0, 1)

    laid_out = {
        "x": w["x"], "ctx": w["ctx_1024"],
        "proj": _np.stack([w["Wk"], w["Wq"], w["Wv"].T], axis=1),
        "gru": _np.stack([turned(w["gru_wih"]), turned(w["gru_whh"])], axis=1),
        "columns": _np.concatenate([w["gru_bih"].reshape(3, D), w["gru_bhh"].reshape(3, D),
                                    w["slot_norm_w"][None], w["input_norm_w"][None]]).T,
        "Wg": w["Wg"], "W1": w["W1"], "b1": w["b1"].reshape(len(w["b1"]), -1, 128).transpose(2, 0, 1), "W2": w["W2"], "b2": w["b2"],
    }
    for name, a in laid_out.items():
        a = _np.ascontiguousarray(a)
        arrays[f"in_{name}"] = a
        args.append(nc.dram_tensor(f"in_{name}", a.shape, _mybir.dt.from_np(a.dtype), kind="ExternalInput").ap())
    out = nc.dram_tensor("out_0", tuple(inputs["x"].shape), F32, kind="ExternalOutput").ap()
    xattn_moe_kernel(nc, *args, out)
    r = _run(nc, [arrays], core_ids=[0])
    return r.results[0]["out_0"]
```

```python
from contextlib import ExitStack

import concourse.bass as bass
from concourse import mybir

F32 = mybir.dt.float32
F32R = mybir.dt.float32r
BF16 = mybir.dt.bfloat16
U32 = mybir.dt.uint32
I32 = mybir.dt.int32
ALU = mybir.AluOpType
ACT = mybir.ActivationFunctionType
AX = mybir.AxisListType

P = 128


def xattn_moe_kernel(nc, x, ctx, proj, gru, columns, Wg, W1, b1, W2, b2, out):
    B, S, D = x.shape
    E, _, F = W1.shape
    TOP = 2
    T = B * S
    CAP = 2 * TOP * T // E
    NTOK = T // P
    GB = 4
    NG = B // GB
    LANES = 4
    ROUNDS = NG // LANES
    ITERS = 3
    FC = F // P
    TILES = TOP * T // P + E - 1
    NJ = TILES + TILES % 2
    SCALE = float(D) ** -0.5
    LOG_P = P.bit_length() - 1
    INVALID = 16384.0

    ln_dram = nc.dram_tensor("ln_rows", [T, D], F32, kind="Internal").ap()
    y_dram = nc.dram_tensor("expert_rows", [TOP * T, D], F32, kind="Internal").ap()
    bias_dram = nc.dram_tensor("bias_parts", [3, E * D], BF16, kind="Internal").ap()

    x_g = x.rearrange("(g b) s d -> g s b d", b=GB)
    ctx_g = ctx.rearrange("(g b) s d -> g s b d", b=GB)
    ln_g = ln_dram.rearrange("(g b s) d -> g s b d", b=GB, s=S)

    with ExitStack() as stack:
        def sb(name, shape, dt=F32):
            return stack.enter_context(nc.sbuf_tensor(name, shape, dt))

        def psum(name):
            return stack.enter_context(nc.psum_tensor(name, [P, 512], F32))

        def sem(name):
            return stack.enter_context(nc.semaphore(name))

        def lane_sems(name):
            return [sem(f"{name}{l}") for l in range(LANES)]

        ident = sb("ident", [P, P])
        ones_col = sb("ones_col", [P, 1])
        ones_bf = sb("ones_bf", [P, P], BF16)
        before = sb("before", [P, P], BF16)
        neg_half = sb("neg_half", [P, GB])
        proj_in = sb("proj_in", [P, 3, D])
        gru_in = sb("gru_in", [P, 2, 3, D])
        col_in = sb("col_in", [P, 8])
        wkq = sb("wkq", [P, D])
        wvT = sb("wvT", [P, D])
        gru_hi = sb("gru_hi", [P, 2, 3, D], F32R)
        gru_lo = sb("gru_lo", [P, 2, 3, D], F32R)
        WIH, WHH = 0, 1
        bias_rz = sb("bias_rz", [P, 2])
        bias_hn = sb("bias_hn", [P, 1])
        slot_scale = sb("slot_scale", [P, 1])
        wg_sb = sb("wg_sb", [P, E])
        w1_sb = sb("w1_sb", [P, E, F + FC])
        w2_sb = sb("w2_sb", [P, E, FC, D])
        w1_now = [sb(f"w1_now{b}", [P, F + FC]) for b in range(2)]
        b_in = sb("b_in", [P, E * D // P])
        b_parts = sb("b_parts", [P, 3, E * D // P], BF16)
        b_rest = sb("b_rest", [P, 2, E * D // P])
        b_rows = sb("b_rows", [P, E * D], BF16)
        unused = sb("unused", [P, GB, D], BF16)
        w1_flat = w1_sb[:, :, :].rearrange("p e f -> p (e f)")
        w2_flat = w2_sb[:, :, :, :].rearrange("p e c d -> p (e c d)")

        c_in = [sb(f"c_in{l}", [P, GB, D]) for l in range(LANES)]
        hT = [sb(f"hT{l}", [P, GB, S]) for l in range(LANES)]
        work = [sb(f"work{l}", [P, GB, P]) for l in range(LANES)]
        prob = [sb(f"prob{l}", [P, GB, S]) for l in range(LANES)]
        tr = [sb(f"tr{l}", [P, GB, S]) for l in range(LANES)]
        tz = [sb(f"tz{l}", [P, GB, S]) for l in range(LANES)]
        hn = [sb(f"hn{l}", [P, GB, S]) for l in range(LANES)]
        kq = [sb(f"kq{l}", [P, GB, P]) for l in range(LANES)]
        v = [sb(f"v{l}", [P, GB, D + 1]) for l in range(LANES)]
        rms = [sb(f"rms{l}", [P, GB]) for l in range(LANES)]
        peak = [sb(f"peak{l}", [P, GB]) for l in range(LANES)]
        uT, h_hi, h_lo, u_hi, u_lo = (
            [sb(f"{name}{l}", [P, GB, S], dt) for l in range(2)] * 2
            for name, dt in (("uT", F32), ("h_hi", F32R), ("h_lo", F32R), ("u_hi", F32R), ("u_lo", F32R)))
        zsum = [sb(f"zsum{l}", [P, GB]) for l in range(LANES)]
        zinv = [sb(f"zinv{l}", [P, GB]) for l in range(LANES)]
        asum = [sb(f"asum{l}", [P, GB]) for l in range(LANES)]
        ainv = [sb(f"ainv{l}", [P, GB]) for l in range(LANES)]
        stats = [sb(f"stats{l}", [P, GB, 6]) for l in range(LANES)]
        moments = [sb(f"moments{l}", [P, GB, 2]) for l in range(LANES)]
        rstd = [sb(f"rstd{l}", [P, GB]) for l in range(LANES)]
        shift = [sb(f"shift{l}", [P, GB]) for l in range(LANES)]
        csum = [sb(f"csum{l}", [P, GB]) for l in range(LANES)]
        crms = [sb(f"crms{l}", [P, GB]) for l in range(LANES)]

        x2 = sb("x2", [P, NTOK, D])
        logits = sb("logits", [P, NTOK, E])
        top8 = sb("top8", [P, NTOK, E])
        top8_at = sb("top8_at", [P, NTOK, E], U32)

        NP = TOP * NTOK
        iota_i = sb("iota_i", [P, P], I32)
        iota_f = sb("iota_f", [P, P])
        iota_b = sb("iota_b", [P, P], BF16)
        row_i = sb("row_i", [P, 1], I32)
        row_f = sb("row_f", [P, 1])
        restart = sb("restart", [P, E, NTOK])
        at = sb("at", [P, TOP, NTOK])
        mask = sb("mask", [P, TOP, E, NTOK], BF16)
        either = sb("either", [P, E, NTOK], BF16)
        upto = sb("upto", [P, E, NTOK])
        place = sb("place", [P, E, NTOK])
        picked = sb("picked", [P, TOP, E, NTOK])
        pos = sb("pos", [P, TOP, NTOK])
        pos_i = sb("pos_i", [P, NP], I32)
        depth_i = sb("depth_i", [P, NP], I32)
        depth = sb("depth", [P, NP])
        in_tile_i = sb("in_tile_i", [P, NP], I32)
        in_tile = sb("in_tile", [P, NP], BF16)
        tiles_i = sb("tiles_i", [P, E], I32)
        tiles_of = sb("tiles_of", [P, E])
        tile_end = sb("tile_end", [P, E])
        tile_base = sb("tile_base", [P, E])
        base_of = sb("base_of", [P, TOP, NTOK])
        which = sb("which", [P, NP], BF16)
        upto_first = sb("upto_first", [P, E, NTOK])
        place_c = sb("place_c", [P, TOP, E, NTOK])
        keep = sb("keep", [P, TOP, NTOK])
        row_far = [sb(f"row_far{b}", [P, 8, P], BF16) for b in range(2)]
        hot_row = [sb(f"hot_row{b}", [P, 8, P], BF16) for b in range(2)]
        hot_tile = [sb(f"hot_tile{b}", [P, 8, NJ], BF16) for b in range(2)]
        hot_value = [sb(f"hot_value{b}", [P, 8, 2 * NJ], BF16) for b in range(2)]
        zero_bf = sb("zero_bf", [P, 2 * NJ], BF16)
        rows_f = sb("rows_f", [P, NJ])
        rows_g = sb("rows_g", [P, NJ])
        rows_e = sb("rows_e", [P, NJ])
        to_rows = sb("to_rows", [P, NJ], U32)
        from_rows = sb("from_rows", [P, NJ], U32)
        ended = sb("ended", [1, NJ, E])
        tile_expert_f = sb("tile_expert_f", [1, NJ])
        tile_expert = sb("tile_expert", [1, NJ], I32)
        exps = sb("exps", [P, NTOK, E])
        exp2 = sb("exp2", [P, NTOK])
        gate = [sb(f"gate{c}", [P, NTOK]) for c in range(TOP)]
        gsum = sb("gsum", [P, NTOK])
        denom = sb("denom", [P, NTOK])

        RB = 4
        from_col = [sb(f"from_col{b}", [P, 1], U32) for b in range(RB)]
        to_col = [sb(f"to_col{b}", [P, 1], U32) for b in range(RB)]
        rows = [sb(f"rows{b}", [P, D]) for b in range(RB)]
        results = [sb(f"results{b}", [P, D]) for b in range(RB)]
        rowsT = [sb(f"rowsT{b}", [P, P]) for b in range(2)]
        hiddenT = tz[0:2]

        lane_bank = [psum(f"lane_bank{l}") for l in range(LANES)]
        bank_r, bank_z, bank_hn, bank_xn = (psum(f"bank_{n}") for n in ("r", "z", "hn", "xn"))

        bank_rows = lane_bank[2:4]
        bank_out = lane_bank[0:2]
        bank_hid = [bank_r, bank_z]

        s_ident, s_const = sem("ident_set"), sem("const_set")
        s_wload, s_gload, s_wmoe, s_bload = sem("w_loaded"), sem("gru_w_loaded"), sem("moe_w_loaded"), sem("bias_loaded")
        s_wp, s_we = sem("w_product"), sem("w_evacuated")
        s_bcol = sem("bias_columns")
        s_bpart, s_bstore, s_brow, s_bzero = (sem("bias_part"), sem("bias_parts_stored"),
                                             sem("bias_rows_loaded"), sem("bias_rows_zeroed"))
        s_iota, s_iotaf = sem("iotas"), sem("iotas_float")
        s_route, s_mask, s_count = sem("routing_step"), sem("mask"), sem("counts")
        s_hott, s_hot, s_hotv, s_far, s_intile, s_hotrow, s_hotuse, s_table, s_texp = (
            sem(n) for n in ("tile_one_hots", "tile_values", "row_values", "row_distances", "row_in_tile", "row_one_hots", "one_hots_used", "table", "tile_expert"))
        s_shift, s_gexp = sem("logits_shifted"), sem("gate_exps")
        s_gate = sem("gates_step")
        s_go = sem("rows_may_move")
        s_fcol, s_tcol = sem("from_column"), sem("to_column")
        s_rows = [sem(f"rows_gathered{b}") for b in range(RB)]
        s_back = [sem(f"rows_scattered{b}") for b in range(RB)]
        s_xp, s_xe, s_w1, s_hp, s_ge, s_yp, s_ye = (
            sem(n) for n in ("rows_turned", "rows_turned_copied", "w1_copied", "hidden_product", "hidden_gelu",
                             "out_product", "out_copied"))
        s_yload = [sem(f"y_loaded{l}") for l in range(LANES)]
        s_first, s_both, s_out = sem("first_choice_added"), sem("both_added"), sem("out_stored")
        s_xload, s_cload = lane_sems("x_loaded"), lane_sems("ctx_loaded")
        s_lnst = lane_sems("ln_stored")
        s_csq, s_cms, s_crms, s_cn, s_cT, s_cTe, s_kq, s_kqe, s_v, s_ve = (
            sem(n) for n in ("ctx_squares", "ctx_mean_square", "ctx_rms", "ctx_normed", "ctx_turned",
                                   "ctx_turned_copied", "kq_product", "kq_copied", "v_product", "v_copied"))
        s_xst, s_xmo, s_xve, s_xrs, s_xnorm, s_xT = (
            sem(n) for n in ("x_stats", "x_moments", "x_variance", "x_rstd", "x_normed", "x_turned"))
        s_h0, s_h = sem("h_started"), sem("h_updated")
        s_sq, s_ssq, s_ms, s_rms, s_sc, s_scs, s_scT = (
            sem(n) for n in ("h_squares", "h_square_sum", "h_mean_square", "h_rms", "scores",
                                   "scores_scaled", "scores_turned"))
        s_pk, s_sub, s_exp, s_zs, s_zi, s_at = (
            sem(n) for n in ("peak", "scores_shifted", "exp", "exp_sum", "exp_inverse", "attn"))
        s_ase, s_ai, s_u, s_un, s_uT, s_uTe = (
            sem(n) for n in ("attn_sum_copied", "attn_inverse", "update_product",
                                   "update_normed", "update_turned", "update_copied"))
        s_R, s_HN, s_Z, s_XN, s_tr, s_hn, s_tz = (
            sem(n) for n in ("r_product", "hn_product", "z_product", "xn_product", "r_tanh", "hn_copied",
                                   "z_tanh"))
        s_fsh = sem("x2_shift")
        s_hhi, s_hlo, s_ulo = sem("h_high_part"), sem("h_low_part"), sem("update_low_part")
        s_rh, s_npre, s_n, s_hmn, s_zh = (
            sem(n) for n in ("r_times_hn", "n_sum", "n_tanh", "h_minus_n", "z_times"))
        s_hf, s_x2, s_fst, s_fmo, s_fve, s_frs, s_fln, s_fT, s_fTe, s_lg, s_lge, s_top, s_topi = (
            sem(n) for n in ("h_turned_back", "x2_ready", "x2_stats", "x2_moments", "x2_variance",
                                   "x2_rstd", "x2_normed", "ln_turned", "ln_turned_copied",
                                   "logits_product", "logits_copied", "top8_found", "top8_indexed"))

        def nth(l, n):
            return LANES * n + l + 1

        def wait_h(eng, l, n):
            if n % ITERS == 0:
                eng.wait_ge(s_h0, nth(l, n // ITERS))
            else:
                eng.wait_ge(s_h, nth(l, n - 1))

        ITER = ["score", "attend", "gates", "update"]
        CYCLE = len(ITER) * ITERS + 1
        LEAD_IN = 3
        SLOTS = LEAD_IN + CYCLE * ROUNDS + LANES + 1

        def slots_of(r):
            start = LEAD_IN + CYCLE * r
            last = r == ROUNDS - 1
            yield "measure", 0, start - (7 if r else 3)
            yield "square", 0, start - (8 if r else 3)
            yield "context", 0, start - (3 if r else 2)
            yield "norm", 0, start - 2
            yield "project", 0, start - (2 if r else 1)
            yield "begin", 0, start - (1 if r else 2)
            for i in range(ITERS):
                for k, stage in enumerate(ITER):
                    yield stage, ITERS * r + i, start + len(ITER) * i + k
            yield "finish", 0, start + CYCLE - 1
            yield "weigh", 0, start + CYCLE - 1 + (0 if last else 2)
            yield "route", 0, start + CYCLE - 1 + (1 if last else 7)
            yield "choose", 0, start + CYCLE - 1 + (2 if last else 8)

        plan = {}
        for l in range(LANES):
            for r in range(ROUNDS):
                for stage, n, at_ in slots_of(r):
                    assert (l + at_, stage) not in plan
                    plan[l + at_, stage] = (l, r, n)

        def so_far(stage, slot):
            return sum(t <= slot and name == stage for t, name in plan)

        def at_slot(slot):
            return {stage: lrn for (t, stage), lrn in plan.items() if t == slot}

        def num(q, w):
            return q * RB + w

        def turn_of(q, w):
            return q + w // RB

        def wait_pos(eng, s, value):
            if not isinstance(value, int) or value > 0:
                eng.wait_ge(s, value)

        LEAD = 4

        def run_tiles(eng, step):
            pairs = ((TILES - 1 - LEAD) // RB - 1) // 2

            def plain(j):
                step(j // RB, j % RB, lambda k: 0 <= j + k < TILES)

            for j in range(RB):
                plain(j)
            with eng.Fori(0, pairs) as h:
                for q in (2 * h + 1, 2 * h + 2):
                    for w in range(RB):
                        step(q, w, lambda k: True)
            for j in range(RB * (2 * pairs + 1), TILES + 1):
                plain(j)

        def group(t, g):
            return t[:, GB * g:GB * g + GB, :]

        def product_of(l, b):
            at = (D + 1) * (b % 3)
            return (lane_bank[l] if b < 3 else bank_z)[:, at:at + D + 1]

        block = stack.enter_context(nc.Block())

        @block.sync
        def _(sp):
            sp.dma_start(proj_in[:, :, :], proj).then_inc(s_wload, 16)
            sp.dma_start(col_in[:, :], columns).then_inc(s_wload, 16)
            sp.dma_start(group(x2, 0), x_g[0]).then_inc(s_xload[0], 16)
            sp.dma_start(c_in[0][:, :, :], ctx_g[0]).then_inc(s_cload[0], 16)
            sp.dma_start(gru_in[:, :, :, :], gru).then_inc(s_gload, 16)
            for l in range(1, LANES):
                sp.dma_start(group(x2, l), x_g[l]).then_inc(s_xload[l], 16)
                sp.dma_start(c_in[l][:, :, :], ctx_g[l]).then_inc(s_cload[l], 16)
            sp.dma_start(wg_sb[:, :], Wg).then_inc(s_wmoe, 16)
            sp.dma_start(w1_sb[:, :, 0:F], W1.rearrange("e d f -> d e f")).then_inc(s_wmoe, 16)
            sp.dma_start(w1_sb[:, :, F:], b1).then_inc(s_wmoe, 16)
            sp.dma_start(w2_sb[:, :, :, :], W2.rearrange("e (c p) d -> p e c d", p=P)).then_inc(s_wmoe, 16)
            sp.dma_start(b_in[:, :], b2.rearrange("e (q n) -> (e q) n", q=P // E)).then_inc(s_bload, 16)
            sp.wait_ge(s_bpart, 5)
            for k in range(3):
                sp.dma_start(bias_dram[k, :].rearrange("(p n) -> p n", p=P), b_parts[:, k, :]).then_inc(s_bstore, 16)
            sp.wait_ge(s_bstore, 48)
            sp.wait_ge(s_bzero, 1)
            sp.dma_start(b_rows[0:3, :], bias_dram).then_inc(s_brow, 16)
            for slot in range(SLOTS):
                now = at_slot(slot)
                if "route" in now:
                    l, r, _ = now["route"]
                    sp.wait_ge(s_fln, nth(l, r))
                    sp.dma_start(ln_g[LANES * r + l], work[l][:, :, :]).then_inc(s_lnst[l], 16)
                if "begin" in now:
                    l, r, _ = now["begin"]
                    if r + 1 < ROUNDS:
                        g = LANES * (r + 1) + l
                        sp.wait_ge(s_cn, nth(l, r))
                        sp.dma_start(c_in[l][:, :, :], ctx_g[g]).then_inc(s_cload[l], 16)
                        sp.wait_ge(s_xst, nth(l, r))
                        sp.dma_start(group(x2, g), x_g[g]).then_inc(s_xload[l], 16)

            for b in range(RB):
                sp.wait_ge(s_back[b], 16 * len(range(b, TILES, RB)))
            y_c = y_dram.rearrange("(c k b s) d -> c k s b d", c=TOP, b=GB, s=P)
            out_g = out.rearrange("(g b) s d -> g s b d", b=GB)

            def load_results(k):
                if k >= LANES:
                    sp.wait_ge(s_both, k - LANES + 1)
                sp.dma_start(v[k % LANES][:, :, 0:D], y_c[0, k]).then_inc(s_yload[k % LANES], 16)
                sp.dma_start(c_in[k % LANES][:, :, :], y_c[1, k]).then_inc(s_yload[k % LANES], 16)

            for k in range(LANES):
                load_results(k)
            for k in range(NG):
                sp.wait_ge(s_both, k + 1)
                sp.dma_start(out_g[k], group(x2, k)).then_inc(s_out, 16)
                if k + LANES < NG:
                    load_results(k + LANES)
            sp.wait_ge(s_out, 16 * NG)

        @block.tensor
        def _(pe):
            pe.wait_ge(s_wload, 32)
            pe.matmul(bank_r[:, 0:P], proj_in[:, 0, :], proj_in[:, 1, :], start=True, stop=True).then_inc(s_wp, 1)
            pe.wait_ge(s_ident, 2)

            def turn(bank, src):
                for b in range(GB):
                    last = pe.transpose(bank[:, b * P:(b + 1) * P], src[:, b, :], ident[:, :])
                return last

            def gate_product(bank, side, gate, hi, lo, start, stop):
                pe.matmul(bank[:, :], gru_hi[:, side, gate, :], hi[:, :, :],
                          start=start, stop=False)
                pe.matmul(bank[:, :], gru_lo[:, side, gate, :], hi[:, :, :],
                          start=False, stop=False)
                return pe.matmul(bank[:, :], gru_hi[:, side, gate, :], lo[:, :, :],
                                 start=False, stop=stop)

            def turn_context(l, r):
                pe.wait_ge(s_cn, nth(l, r))
                if r:
                    pe.wait_ge(s_uTe, nth(l, ITERS * r - 1))
                turn(lane_bank[l], work[l]).then_inc(s_cT, 1)

            def turn_x(l, r):
                pe.wait_ge(s_xnorm, nth(l, r))
                if r:
                    pe.wait_ge(s_x2, nth(l, r - 1))
                    turn(lane_bank[l], work[l]).then_inc(s_xT, 1)
                else:
                    if l:
                        pe.wait_ge(s_h0, l)
                    turn(bank_hn, uT[l]).then_inc(s_xT, 1)

            def project_kq(l, r, _):
                pe.wait_ge(s_cTe, nth(l, r))
                pe.wait_ge(s_we, 3)
                pe.matmul(lane_bank[l][:, :], wkq[:, :], prob[l][:, :, :], start=True, stop=True)\
                    .then_inc(s_kq, 1)

            for slot in range(SLOTS):
                now = at_slot(slot)
                score, attend, gates = now.get("score"), now.get("attend"), now.get("gates")
                context, project, begin = now.get("context"), now.get("project"), now.get("begin")
                finish, route = now.get("finish"), now.get("route")
                if finish:
                    l, r, _ = finish
                    pe.wait_ge(s_h, nth(l, ITERS * r + ITERS - 1))
                    if r + 1 < ROUNDS:
                        pe.wait_ge(s_ve, nth(l, r + 1))
                    turn(lane_bank[l], hT[l]).then_inc(s_hf, 1)
                if project and not project[1]:
                    project_kq(*project)
                if gates:
                    l, _, n = gates
                    if l or n:
                        pe.wait_ge(s_tr, nth(l, n) - 1)
                    if n == 0:
                        pe.wait_ge(s_we, 6)
                        pe.wait_ge(s_h0, LANES)
                    pe.wait_ge(s_hlo, nth(l, n))
                    gate_product(bank_r, WHH, 0, h_hi[l], h_lo[l], start=True, stop=False)
                if score:
                    l, _, n = score
                    pe.wait_ge(s_sq, nth(l, n))
                    for b in range(GB):
                        last = pe.matmul(lane_bank[l][:, b:b + 1], work[l][:, b, :], ones_col[:, :],
                                         start=True, stop=True)
                    last.then_inc(s_ssq, 1)
                if begin and not begin[1]:
                    turn_x(*begin[0:2])
                if context and not context[1]:
                    turn_context(*context[0:2])
                if project and project[1]:
                    project_kq(*project)
                if score:
                    l, _, n = score
                    pe.wait_ge(s_ms, nth(l, n))
                    for b in range(GB):
                        last = pe.matmul(lane_bank[l][:, b * P:(b + 1) * P], hT[l][:, b, :], kq[l][:, b, :],
                                         start=True, stop=True)
                    last.then_inc(s_sc, 1)
                if attend:
                    l, _, n = attend
                    pe.wait_ge(s_at, nth(l, n))
                    if so_far("gates", slot - 1):
                        pe.wait_ge(s_tz, so_far("gates", slot - 1))
                    for b in range(GB):
                        last = pe.matmul(product_of(l, b), prob[l][:, b, :], v[l][:, b, :], start=True, stop=True)
                    last.then_inc(s_u, 1)
                if score:
                    l, _, n = score
                    pe.wait_ge(s_scs, nth(l, n))
                    turn(lane_bank[l], work[l]).then_inc(s_scT, 1)
                if gates:
                    l, _, n = gates
                    pe.wait_ge(s_ulo, nth(l, n))
                    gate_product(bank_r, WIH, 0, u_hi[l], u_lo[l], start=False, stop=True)\
                        .then_inc(s_R, 1)
                if gates:
                    l, _, n = gates
                    if l or n:
                        pe.wait_ge(s_hn, nth(l, n) - 1)
                    gate_product(bank_hn, WHH, 2, h_hi[l], h_lo[l], start=True, stop=True)\
                        .then_inc(s_HN, 1)
                if route:
                    l, r, _ = route
                    pe.wait_ge(s_fln, nth(l, r))
                    turn(lane_bank[l], work[l]).then_inc(s_fT, 1)
                if context and context[1]:
                    turn_context(*context[0:2])
                if project:
                    l, r, _ = project
                    pe.wait_ge(s_kqe, nth(l, r))
                    for b in range(GB):
                        last = pe.matmul(lane_bank[l][:, b * D:(b + 1) * D], prob[l][:, b, :], wvT[:, :],
                                         start=True, stop=True)
                    last.then_inc(s_v, 1)
                if begin and begin[1]:
                    turn_x(*begin[0:2])
                if attend:
                    l, _, n = attend
                    pe.wait_ge(s_un, nth(l, n))
                    turn(lane_bank[l], work[l]).then_inc(s_uT, 1)
                if gates:
                    l, _, n = gates
                    pe.wait_ge(s_un, so_far("attend", slot))
                    if l or n:
                        pe.wait_ge(s_tz, nth(l, n) - 1)
                    gate_product(bank_z, WHH, 1, h_hi[l], h_lo[l], start=True, stop=False)
                    gate_product(bank_z, WIH, 1, u_hi[l], u_lo[l], start=False, stop=True)\
                        .then_inc(s_Z, 1)
                if route:
                    l, r, _ = route
                    pe.wait_ge(s_fTe, nth(l, r))
                    pe.wait_ge(s_wmoe, 64)
                    for b in range(GB):
                        last = pe.matmul(lane_bank[l][:, b * E:(b + 1) * E], prob[l][:, b, :], wg_sb[:, :],
                                         start=True, stop=True)
                    last.then_inc(s_lg, 1)
                if gates:
                    l, _, n = gates
                    if l or n:
                        pe.wait_ge(s_npre, nth(l, n) - 1)
                    gate_product(bank_xn, WIH, 2, u_hi[l], u_lo[l], start=True, stop=True)\
                        .then_inc(s_XN, 1)
            pe.wait_ge(s_const, 2)
            pe.wait_ge(s_mask, 3)
            for counted, bank in ((either, bank_hid[0]), (mask[:, 0], bank_xn)):
                pe.matmul(bank[:, 0:E * NTOK], before[:, :], counted[:, :, :], start=True, stop=True)
                pe.matmul(bank[:, E * NTOK:2 * E * NTOK], ones_bf[:, :], counted[:, :, :],
                          start=True, stop=True).then_inc(s_count, 1)
            table = bank_hn[:, 0:2 * NJ]
            pe.wait_ge(s_iotaf, 5)
            pe.matmul(table, zero_bf[:, 0:P], zero_bf[:, :], start=True, stop=False).then_inc(s_hotuse, 2)
            with pe.Fori(0, NP // 16) as q:
                for b in range(2):
                    pe.wait_ge(s_hot, 2 * q + b + 1)
                    pe.wait_ge(s_hotv, 2 * q + b + 1)
                    pe.wait_ge(s_hotrow, 2 * q + b + 1)
                    for i in range(8):
                        last = pe.matmul(table, hot_row[b][:, i, :], hot_value[b][:, i, :],
                                         start=False, stop=False)
                    last.then_inc(s_hotuse, 1)
            pe.matmul(table, zero_bf[:, 0:P], zero_bf[:, :], start=False, stop=True).then_inc(s_table, 1)

            pe.wait_ge(s_brow, 16)
            pe.wait_ge(s_texp, 1)

            def turn_rows(q, w):
                pe.wait_ge(s_rows[w % RB], 16 * (turn_of(q, w) + 1))
                wait_pos(pe, s_xe, num(q, w) - 1)
                pe.transpose(bank_rows[w % 2][:, 0:P], rows[w % RB][:, :], ident[:, :]).then_inc(s_xp, 1)

            def first_layer(q, w):
                pe.wait_ge(s_w1, num(q, w) + 1)
                pe.wait_ge(s_xe, num(q, w) + 1)
                wait_pos(pe, s_ge, num(q, w) - 1)
                for c in range(FC):
                    last = pe.matmul(bank_hid[w % 2][:, c * P:(c + 1) * P], w1_now[w % 2][:, c * P:(c + 1) * P],
                                     rowsT[w % 2][:, :], start=True, stop=True)
                last.then_inc(s_hp, 1)

            def second_layer(q, w):
                e = pe.value_load(tile_expert[0:1, bass.ds(num(q, w), 1)], min_val=0, max_val=E - 1)
                pe.wait_ge(s_ge, num(q, w) + 1)
                wait_pos(pe, s_ye, num(q, w) - 1)
                pe.matmul(bank_out[w % 2][:, 0:D], ones_bf[:, :], b_rows[:, bass.ds(e * D, D)],
                          start=True, stop=False)
                for c in range(FC):
                    last = pe.matmul(bank_out[w % 2][:, 0:D], hiddenT[w % 2][:, c, :],
                                     w2_flat[:, bass.ds(e * F + c * D, D)], start=False, stop=(c == FC - 1))
                last.then_inc(s_yp, 1)

            turn_rows(0, 0)
            turn_rows(0, 1)
            first_layer(0, 0)

            def pe_step(q, w, has):
                if has(1):
                    first_layer(q, w + 1)
                if has(2):
                    turn_rows(q, w + 2)
                if has(0):
                    second_layer(q, w)

            run_tiles(pe, pe_step)

        @block.scalar
        def _(act):
            def copy_context(l, r):
                act.wait_ge(s_cT, nth(l, r))
                act.activation(prob[l][:, :, :], lane_bank[l][:, :], ACT.Copy).then_inc(s_cTe, 1)

            def copy_x(l, r):
                act.wait_ge(s_xT, nth(l, r))
                act.activation(hT[l][:, :, :], (lane_bank[l] if r else bank_hn)[:, :], ACT.Copy).then_inc(s_h0, 1)

            def copy_kq(l, r, _):
                act.wait_ge(s_kq, nth(l, r))
                act.wait_ge(s_bcol, 3)
                act.activation(kq[l][:, :, :], lane_bank[l][:, :], ACT.Copy, scale=slot_scale[:, :])\
                    .then_inc(s_kqe, 1)

            for slot in range(SLOTS):
                now = at_slot(slot)
                score, attend, gates, update = (now.get(k) for k in ITER)
                gates_before = at_slot(slot - 1).get("gates")
                context, project, begin = now.get("context"), now.get("project"), now.get("begin")
                square, route = now.get("square"), now.get("route")
                if score:
                    l, r, n = score
                    wait_h(act, l, n)
                    if r and n == ITERS * r + 2:
                        act.wait_ge(s_lnst[l], 16 * r)
                    act.activation(work[l][:, :, :], hT[l][:, :, :], ACT.Square).then_inc(s_sq, 1)
                if gates_before:
                    l, _, n = gates_before
                    act.wait_ge(s_Z, nth(l, n))
                    act.activation(tz[l][:, :, :], bank_z[:, :], ACT.Tanh, bias=bias_rz[:, 1:2], scale=0.5)\
                        .then_inc(s_tz, 1)
                if attend:
                    l, _, n = attend
                    wait_h(act, l, n)
                    if nth(l, n) > 2:
                        act.wait_ge(s_Z, nth(l, n) - 2)
                    act.activation(h_hi[l][:, :, :], hT[l][:, :, :], ACT.Copy).then_inc(s_hhi, 1)
                if square:
                    l, r, _ = square
                    act.wait_ge(s_cload[l], 16 * (r + 1))
                    if l or r:
                        act.wait_ge(s_csq, nth(l, r) - 1)
                    for b in range(GB):
                        last = act.activation(unused[:, b, :], c_in[l][:, b, :], ACT.Square,
                                              accum_out=csum[l][:, b:b + 1])
                    last.then_inc(s_csq, 1)
                if project and not project[1]:
                    copy_kq(*project)
                if begin and not begin[1]:
                    copy_x(*begin[0:2])
                if context and not context[1]:
                    copy_context(*context[0:2])
                if route and route[1] + 1 < ROUNDS:
                    l, r, _ = route
                    act.wait_ge(s_fsh, nth(l, r))
                    act.wait_ge(s_uT, nth(l, ITERS * (r + 1) + 1))
                    for b in range(GB):
                        last = act.activation(work[l][:, b, :], x2[:, GB * (LANES * r + l) + b, :], ACT.Identity,
                                              bias=shift[l][:, b:b + 1], scale=rstd[l][:, b:b + 1])
                    last.then_inc(s_fln, 1)
                if update:
                    l, _, n = update
                    act.wait_ge(s_npre, nth(l, n))
                    act.activation(tr[l][:, :, :], tr[l][:, :, :], ACT.Tanh, bias=col_in[:, 2:3])\
                        .then_inc(s_n, 1)
                if project and project[1]:
                    copy_kq(*project)
                if gates:
                    l, _, n = gates
                    act.wait_ge(s_R, nth(l, n))
                    if n == 0:
                        act.wait_ge(s_bcol, 3)
                    act.activation(tr[l][:, :, :], bank_r[:, :], ACT.Tanh, bias=bias_rz[:, 0:1], scale=0.5)\
                        .then_inc(s_tr, 1)
                    act.wait_ge(s_HN, nth(l, n))
                    act.activation(hn[l][:, :, :], bank_hn[:, :], ACT.Identity, bias=bias_hn[:, :])\
                        .then_inc(s_hn, 1)
                if context and context[1]:
                    copy_context(*context[0:2])
                if begin and begin[1]:
                    copy_x(*begin[0:2])
                if project:
                    l, r, _ = project
                    act.wait_ge(s_v, nth(l, r))
                    act.activation(v[l][:, :, 0:D], lane_bank[l][:, :].rearrange("p (b d) -> p b d", b=GB), ACT.Copy)\
                        .then_inc(s_ve, 1)
                if route:
                    l, r, _ = route
                    act.wait_ge(s_fT, nth(l, r))
                    act.activation(prob[l][:, :, :], lane_bank[l][:, :], ACT.Copy).then_inc(s_fTe, 1)
                if attend:
                    l, _, n = attend
                    act.wait_ge(s_uT, nth(l, n))
                    act.activation(uT[l][:, :, :], lane_bank[l][:, :], ACT.Copy)
                    if nth(l, n) > 2:
                        act.wait_ge(s_XN, nth(l, n) - 2)
                    act.activation(u_hi[l][:, :, :], lane_bank[l][:, :], ACT.Copy)\
                        .then_inc(s_uTe, 1)
                if score:
                    l, _, n = score
                    act.wait_ge(s_sub, nth(l, n))
                    act.activation(prob[l][:, :, :], prob[l][:, :, :], ACT.Exp).then_inc(s_exp, 1)

            act.wait_ge(s_shift, 2)
            act.activation(exps[:, :, :], exps[:, :, :], ACT.Exp).then_inc(s_gexp, 1)
            act.activation(exp2[:, :], exp2[:, :], ACT.Exp).then_inc(s_gexp, 1)

            for k in range(NP // 8):
                act.wait_ge(s_hott, k + 1)
                act.wait_ge(s_hotuse, k + 1)
                act.activation(hot_value[k % 2][:, :, NJ:2 * NJ], hot_tile[k % 2][:, :, :], ACT.Copy,
                               scale=row_f[:, :]).then_inc(s_hotv, 1)

            def copy_rows(q, w):
                act.wait_ge(s_xp, num(q, w) + 1)
                wait_pos(act, s_hp, num(q, w) - 1)
                act.activation(rowsT[w % 2][:, :], bank_rows[w % 2][:, 0:P], ACT.Copy).then_inc(s_xe, 1)

            def gelu(q, w):
                act.wait_ge(s_hp, num(q, w) + 1)
                wait_pos(act, s_yp, num(q, w) - 1)
                for c in range(FC):
                    last = act.activation(hiddenT[w % 2][:, c, :], bank_hid[w % 2][:, c * P:(c + 1) * P], ACT.Gelu,
                                          bias=w1_now[w % 2][:, F + c:F + c + 1])
                last.then_inc(s_ge, 1)

            copy_rows(0, 0)
            copy_rows(0, 1)

            def act_step(q, w, has):
                if has(0):
                    gelu(q, w)
                if has(2):
                    copy_rows(q, w + 2)

            run_tiles(act, act_step)

        @block.vector
        def _(dve):
            def spread(column):
                return column[:, :].unsqueeze(2).to_broadcast([P, GB, P])

            def bank3(bank):
                return bank[:, :].rearrange("p (b s) -> p b s", b=GB)

            def first3(l):
                return lane_bank[l][:, 0:3 * (D + 1)].rearrange("p (b d) -> p b d", b=3)

            dve.wait_ge(s_wload, 32)
            dve.tensor_tensor(bias_rz[:, :], col_in[:, 0:2], col_in[:, 3:5], ALU.add).then_inc(s_we, 1)
            dve.wait_ge(s_we, 1)
            dve.tensor_scalar(bias_rz[:, :], bias_rz[:, :], 0.5, None, ALU.mult).then_inc(s_bcol, 1)
            dve.tensor_scalar(bias_hn[:, :], col_in[:, 5:6], 0.5, None, ALU.mult).then_inc(s_bcol, 1)
            dve.tensor_scalar(slot_scale[:, :], col_in[:, 6:7], SCALE, None, ALU.mult).then_inc(s_bcol, 1)
            dve.tensor_scalar(wvT[:, :], proj_in[:, 2, :], col_in[:, 7:8], None, ALU.mult).then_inc(s_we, 1)
            dve.wait_ge(s_wp, 1)
            dve.tensor_scalar(wkq[:, :], bank_r[:, 0:P], col_in[:, 7:8], None, ALU.mult).then_inc(s_we, 1)
            def gru_parts():
                dve.wait_ge(s_gload, 16)
                dve.tensor_scalar(gru_in[:, WHH, 2, :], gru_in[:, WHH, 2, :], 0.5, None, ALU.mult).then_inc(s_we, 1)
                dve.wait_ge(s_we, 4)
                dve.tensor_copy(gru_hi[:, :, :, :], gru_in[:, :, :, :]).then_inc(s_we, 1)
                dve.wait_ge(s_we, 5)
                dve.tensor_tensor(gru_lo[:, :, :, :], gru_in[:, :, :, :], gru_hi[:, :, :, :].bitcast(F32),
                                  ALU.subtract).then_inc(s_we, 1)

            def bias_parts():
                dve.wait_ge(s_bload, 16)
                dve.tensor_copy(b_parts[:, 0, :], b_in[:, :]).then_inc(s_bpart, 1)
                dve.wait_ge(s_bpart, 1)
                dve.tensor_tensor(b_rest[:, 0, :], b_in[:, :], b_parts[:, 0, :], ALU.subtract).then_inc(s_bpart, 1)
                dve.wait_ge(s_bpart, 2)
                dve.tensor_copy(b_parts[:, 1, :], b_rest[:, 0, :]).then_inc(s_bpart, 1)
                dve.wait_ge(s_bpart, 3)
                dve.tensor_tensor(b_rest[:, 1, :], b_rest[:, 0, :], b_parts[:, 1, :], ALU.subtract)\
                    .then_inc(s_bpart, 1)
                dve.wait_ge(s_bpart, 4)
                dve.tensor_copy(b_parts[:, 2, :], b_rest[:, 1, :]).then_inc(s_bpart, 1)

            def moments_of(g, l, times, st, mo, ve):
                for b in range(GB):
                    last = dve.bn_stats(stats[l][:, b, :], x2[:, GB * g + b, :])
                last.then_inc(st, 1)
                dve.wait_ge(st, times)
                for b in range(GB):
                    last = dve.bn_aggr(moments[l][:, b, :], stats[l][:, b, :])
                last.then_inc(mo, 1)
                dve.wait_ge(mo, times)
                dve.tensor_scalar(rstd[l][:, :], moments[l][:, :, 1], 1e-5, None, ALU.add).then_inc(ve, 1)

            def normed(g, l, to, done):
                for b in range(GB):
                    last = dve.tensor_scalar(to[:, b, :], x2[:, GB * g + b, :], moments[l][:, b, 0:1],
                                             rstd[l][:, b:b + 1], ALU.subtract, ALU.mult)
                last.then_inc(done, 1)

            def norm_x2(l, r, _):
                dve.wait_ge(s_frs, nth(l, r))
                dve.wait_ge(s_uT, nth(l, ITERS * (r + 1) - 1))
                normed(LANES * r + l, l, work[l], s_fln)

            def mean_square(l, r, _):
                dve.wait_ge(s_csq, nth(l, r))
                dve.tensor_scalar(crms[l][:, :], csum[l][:, :], 1.0 / D, 1e-6, ALU.mult, ALU.add)\
                    .then_inc(s_cms, 1)

            def measure_x(l, r, _):
                dve.wait_ge(s_xload[l], 16 * (r + 1))
                moments_of(LANES * r + l, l, nth(l, r), s_xst, s_xmo, s_xve)

            def norm_x(l, r, _):
                dve.wait_ge(s_xrs, nth(l, r))
                if r:
                    dve.wait_ge(s_cT, nth(l, r))
                elif l >= 2:
                    dve.wait_ge(s_xT, l - 1)
                normed(LANES * r + l, l, work[l] if r else uT[l], s_xnorm)

            def choose_experts(l, r, _):
                g = LANES * r + l
                dve.wait_ge(s_lg, nth(l, r))
                dve.tensor_copy(group(logits, g),
                                lane_bank[l][:, 0:GB * E].rearrange("p (b e) -> p b e", b=GB))\
                    .then_inc(s_lge, 1)
                dve.wait_ge(s_lge, nth(l, r))
                for b in range(GB):
                    last = dve.max(top8[:, GB * g + b, :], logits[:, GB * g + b, :])
                last.then_inc(s_top, 1)
                dve.wait_ge(s_top, nth(l, r))
                for b in range(GB):
                    last = dve.max_index(top8_at[:, GB * g + b, :], top8[:, GB * g + b, :],
                                         logits[:, GB * g + b, :])
                last.then_inc(s_topi, 1)

            for slot in range(SLOTS):
                now = at_slot(slot)
                score, attend, update = now.get("score"), now.get("attend"), now.get("update")
                measure, square, context = now.get("measure"), now.get("square"), now.get("context")
                norm, finish, weigh = now.get("norm"), now.get("finish"), now.get("weigh")
                route, choose = now.get("route"), now.get("choose")
                if slot == 3:
                    gru_parts()
                if slot == 6:
                    bias_parts()
                if route and route[1] + 1 < ROUNDS:
                    l, r, _ = route
                    dve.wait_ge(s_frs, nth(l, r))
                    dve.scalar_tensor_tensor(shift[l][:, :], moments[l][:, :, 0], -1.0, rstd[l][:, :],
                                             ALU.mult, ALU.mult).then_inc(s_fsh, 1)
                if attend:
                    l, _, n = attend
                    dve.wait_ge(s_exp, nth(l, n))
                    dve.tensor_reduce(zsum[l][:, :], prob[l][:, :, :], AX.X, ALU.add).then_inc(s_zs, 1)
                    dve.wait_ge(s_zs, nth(l, n))
                    dve.reciprocal(zinv[l][:, :], zsum[l][:, :]).then_inc(s_zi, 1)
                if finish:
                    l, r, _ = finish
                    xg = group(x2, LANES * r + l)
                    dve.wait_ge(s_hf, nth(l, r))
                    dve.tensor_tensor(xg, bank3(lane_bank[l]), xg, ALU.add).then_inc(s_x2, 1)
                if update:
                    l, _, n = update
                    dve.wait_ge(s_tr, nth(l, n))
                    dve.wait_ge(s_hn, nth(l, n))
                    dve.scalar_tensor_tensor(tr[l][:, :, :], tr[l][:, :, :], 1.0, hn[l][:, :, :],
                                             ALU.add, ALU.mult).then_inc(s_rh, 1)
                if score:
                    l, _, n = score
                    dve.wait_ge(s_ssq, nth(l, n))
                    dve.tensor_scalar(rms[l][:, :], lane_bank[l][:, 0:GB], 1.0 / D, 1e-6, ALU.mult, ALU.add)\
                        .then_inc(s_ms, 1)
                if update:
                    l, _, n = update
                    dve.wait_ge(s_rh, nth(l, n))
                    dve.wait_ge(s_XN, nth(l, n))
                    dve.tensor_tensor(tr[l][:, :, :], tr[l][:, :, :], bank3(bank_xn), ALU.add)\
                        .then_inc(s_npre, 1)
                if context:
                    l, r, _ = context
                    dve.wait_ge(s_crms, nth(l, r))
                    dve.tensor_tensor(work[l][:, :, :], c_in[l][:, :, :], spread(crms[l]), ALU.mult)\
                        .then_inc(s_cn, 1)
                if norm and not norm[1]:
                    norm_x(*norm)
                if measure:
                    measure_x(*measure)
                if square:
                    mean_square(*square)
                if choose and choose[1] + 1 < ROUNDS:
                    choose_experts(*choose)
                if route and route[1] + 1 == ROUNDS:
                    norm_x2(*route)
                if weigh:
                    l, r, _ = weigh
                    dve.wait_ge(s_x2, nth(l, r))
                    moments_of(LANES * r + l, l, nth(l, r), s_fst, s_fmo, s_fve)
                if score:
                    l, _, n = score
                    dve.wait_ge(s_sc, nth(l, n))
                    dve.wait_ge(s_rms, nth(l, n))
                    dve.tensor_tensor(work[l][:, :, :], bank3(lane_bank[l]), spread(rms[l]), ALU.mult)\
                        .then_inc(s_scs, 1)
                if attend:
                    l, _, n = attend
                    dve.wait_ge(s_u, nth(l, n))
                    dve.tensor_scalar(asum[l][:, 0:3], first3(l)[:, :, D], 1e-6, None, ALU.add)
                    dve.tensor_scalar(asum[l][:, 3:4], product_of(l, 3)[:, D:D + 1], 1e-6, None, ALU.add)\
                        .then_inc(s_ase, 1)
                    dve.wait_ge(s_ase, nth(l, n))
                    dve.reciprocal(ainv[l][:, :], asum[l][:, :]).then_inc(s_ai, 1)
                    dve.wait_ge(s_ai, nth(l, n))
                    dve.tensor_tensor(work[l][:, 0:3, :], first3(l)[:, :, 0:D],
                                      ainv[l][:, 0:3].unsqueeze(2).to_broadcast([P, 3, D]), ALU.mult)
                    dve.tensor_scalar(work[l][:, 3, :], product_of(l, 3)[:, 0:D], ainv[l][:, 3:4], None, ALU.mult)\
                        .then_inc(s_un, 1)
                if score:
                    l, _, n = score
                    dve.wait_ge(s_scT, nth(l, n))
                    dve.tensor_reduce(peak[l][:, :], bank3(lane_bank[l]), AX.X, ALU.max).then_inc(s_pk, 1)
                    dve.wait_ge(s_pk, nth(l, n))
                    dve.tensor_tensor(prob[l][:, :, :], bank3(lane_bank[l]), spread(peak[l]), ALU.subtract)\
                        .then_inc(s_sub, 1)
                if update:
                    l, _, n = update
                    dve.wait_ge(s_hmn, nth(l, n))
                    dve.wait_ge(s_tz, nth(l, n))
                    dve.scalar_tensor_tensor(hn[l][:, :, :], tz[l][:, :, :], 1.0, hn[l][:, :, :],
                                             ALU.add, ALU.mult).then_inc(s_zh, 1)
                    dve.wait_ge(s_zh, nth(l, n))
                    dve.scalar_tensor_tensor(hT[l][:, :, :], hn[l][:, :, :], 0.5, tr[l][:, :, :],
                                             ALU.mult, ALU.add).then_inc(s_h, 1)
                if norm and norm[1]:
                    norm_x(*norm)
                if choose and choose[1] + 1 == ROUNDS:
                    choose_experts(*choose)

            steps = [0]

            def link(ins):
                steps[0] += 1
                ins.then_inc(s_route, 1)
                dve.wait_ge(s_route, steps[0])

            def per_token(t):
                return t.unsqueeze(1).to_broadcast([P, E, NTOK])

            def per_expert(t):
                return t.unsqueeze(2).to_broadcast([P, E, NTOK])

            dve.wait_ge(s_topi, NG)
            dve.wait_ge(s_iotaf, 5)
            for c in range(TOP):
                link(dve.tensor_copy(at[:, c, :], top8_at[:, :, c]))
            for c in range(TOP):
                dve.tensor_tensor(mask[:, c], per_token(at[:, c, :]), per_expert(iota_f[:, 0:E]), ALU.is_equal)\
                    .then_inc(s_mask, 1)
            dve.wait_ge(s_mask, 2)
            dve.tensor_tensor(either[:, :, :], mask[:, 0], mask[:, 1], ALU.add).then_inc(s_mask, 1)
            dve.tensor_tensor(exps[:, :, :], logits[:, :, :], top8[:, :, 0:1].to_broadcast([P, NTOK, E]),
                              ALU.subtract).then_inc(s_shift, 1)
            dve.tensor_tensor(exp2[:, :], top8[:, :, 1], top8[:, :, 0], ALU.subtract).then_inc(s_shift, 1)
            def places(to, running, bank):
                in_tile_count = bank[:, 0:E * NTOK].rearrange("p (e t) -> p e t", e=E)
                total = bank[:, E * NTOK:2 * E * NTOK]
                link(dve.tensor_tensor_scan(running.rearrange("p e t -> p (e t)"),
                                            restart[:, :, :].rearrange("p e t -> p (e t)"), total, 0.0,
                                            ALU.mult, ALU.add))
                link(dve.tensor_tensor(to, running, total.rearrange("p (e t) -> p e t", e=E), ALU.subtract))
                link(dve.tensor_tensor(to, to, in_tile_count, ALU.add))

            def pick(to, of):
                link(dve.tensor_tensor(picked[:, :, :, :], of, mask[:, :, :, :], ALU.mult))
                link(dve.tensor_reduce(to, picked[:, :, :, :].rearrange("p c e t -> p c t e"), AX.X, ALU.add))

            dve.wait_ge(s_count, 1)
            places(place[:, :, :], upto[:, :, :], bank_hid[0])
            pick(pos[:, :, :], place[:, :, :].unsqueeze(1).to_broadcast([P, TOP, E, NTOK]))
            link(dve.tensor_copy(pos_i[:, :], pos[:, :, :].rearrange("p c t -> p (c t)")))
            link(dve.tensor_scalar(in_tile_i[:, :], pos_i[:, :], P - 1, None, ALU.bitwise_and))
            dve.tensor_copy(in_tile[:, :], in_tile_i[:, :]).then_inc(s_intile, 1)
            link(dve.tensor_scalar(depth_i[:, :], pos_i[:, :], LOG_P, None, ALU.arith_shift_right))
            link(dve.tensor_copy(depth[:, :], depth_i[:, :]))
            link(dve.tensor_scalar(tiles_i[:, :], upto[:, :, NTOK - 1], float(P - 1), None, ALU.add))
            link(dve.tensor_scalar(tiles_i[:, :], tiles_i[:, :], LOG_P, None, ALU.arith_shift_right))
            link(dve.tensor_copy(tiles_of[:, :], tiles_i[:, :]))
            link(dve.tensor_tensor_scan(tile_end[:, :], restart[:, 0, 1:1 + E], tiles_of[:, :], 0.0,
                                        ALU.mult, ALU.add))
            link(dve.tensor_tensor(tile_base[:, :], tile_end[:, :], tiles_of[:, :], ALU.subtract))
            pick(base_of[:, :, :], tile_base[:, :].unsqueeze(1).unsqueeze(3).to_broadcast([P, TOP, E, NTOK]))
            link(dve.tensor_tensor(which[:, :], depth[:, :], base_of[:, :, :].rearrange("p c t -> p (c t)"), ALU.add))
            with dve.Fori(0, NP // 16) as q:
                for b in range(2):
                    dve.wait_ge(s_hotuse, 2 * q + b + 1)
                    pairs = bass.ds(16 * q + 8 * b, 8)
                    dve.tensor_tensor(hot_tile[b][:, :, :], which[:, pairs].unsqueeze(2).to_broadcast([P, 8, NJ]),
                                      iota_b[:, 0:NJ].unsqueeze(1).to_broadcast([P, 8, NJ]), ALU.is_equal)\
                        .then_inc(s_hott, 1)
                    dve.wait_ge(s_far, 2 * q + b + 1)
                    dve.tensor_scalar(hot_row[b][:, :, :], row_far[b][:, :, :], 0.0, None, ALU.is_equal)\
                        .then_inc(s_hotrow, 1)
                    dve.wait_ge(s_hott, 2 * q + b + 1)
                    dve.tensor_tensor(hot_value[b][:, :, 0:NJ], hot_tile[b][:, :, :],
                                      iota_b[:, bass.ds(16 * q + 8 * b + 1, 8)].unsqueeze(2)
                                      .to_broadcast([P, 8, NJ]), ALU.mult).then_inc(s_hot, 1)
            dve.tensor_tensor(ended[:, :, :], tile_end[0:1, :].unsqueeze(1).to_broadcast([1, NJ, E]),
                              iota_f[0:1, 0:NJ].unsqueeze(2).to_broadcast([1, NJ, E]), ALU.is_le)\
                .then_inc(s_gate, 1)
            dve.wait_ge(s_gate, 1)
            dve.tensor_reduce(tile_expert_f[:, :], ended[:, :, :], AX.X, ALU.add).then_inc(s_gate, 1)
            dve.wait_ge(s_gate, 2)
            dve.tensor_scalar(tile_expert[:, :], tile_expert_f[:, :], float(E - 1), None, ALU.min)\
                .then_inc(s_texp, 1)
            table_tile, table_row = bank_hn[:, 0:NJ], bank_hn[:, NJ:2 * NJ]
            dve.wait_ge(s_table, 1)
            link(dve.tensor_scalar(rows_f[:, :], table_tile, float(P), -float(P), ALU.mult, ALU.add))
            link(dve.tensor_tensor(rows_f[:, :], rows_f[:, :], table_row, ALU.add))
            link(dve.tensor_scalar(rows_g[:, :], rows_f[:, :], float(T), -float(T), ALU.is_ge, ALU.mult))
            link(dve.tensor_tensor(rows_g[:, :], rows_g[:, :], rows_f[:, :], ALU.add))
            link(dve.tensor_scalar(from_rows[:, :], rows_g[:, :], 0.0, None, ALU.max))

            def from_column(q, w):
                if not (isinstance(q, int) and turn_of(q, w) == 0):
                    dve.wait_ge(s_rows[w % RB], 16 * turn_of(q, w))
                dve.tensor_copy(from_col[w % RB][:, :], from_rows[:, bass.ds(num(q, w), 1)]).then_inc(s_fcol, 1)

            def to_column(q, w):
                if not (isinstance(q, int) and turn_of(q, w) == 0):
                    dve.wait_ge(s_back[w % RB], 16 * turn_of(q, w))
                dve.tensor_copy(to_col[w % RB][:, :], to_rows[:, bass.ds(num(q, w), 1)]).then_inc(s_tcol, 1)

            def copy_w1(q, w):
                e = dve.value_load(tile_expert[0:1, bass.ds(num(q, w), 1)], min_val=0, max_val=E - 1)
                wait_pos(dve, s_ge, num(q, w) - 1)
                wait_pos(dve, s_hp, num(q, w) - 1)
                dve.tensor_copy(w1_now[w % 2][:, :], w1_flat[:, bass.ds(e * (F + FC), F + FC)]).then_inc(s_w1, 1)

            def copy_results(q, w):
                dve.wait_ge(s_yp, num(q, w) + 1)
                dve.tensor_copy(results[w % RB][:, :], bank_out[w % 2][:, 0:D]).then_inc(s_ye, 1)

            for j in range(LEAD):
                from_column(0, j)
            link(dve.tensor_scalar(rows_e[:, :], table_tile, 0.0, INVALID, ALU.is_equal, ALU.mult))
            link(dve.tensor_tensor(to_rows[:, :], rows_f[:, :], rows_e[:, :], ALU.add))
            dve.wait_ge(s_texp, 1)
            for j in range(2):
                copy_w1(0, j)
            dve.wait_ge(s_count, 2)
            places(place_c[:, 0], upto_first[:, :, :], bank_xn)
            link(dve.tensor_tensor(place_c[:, 1], place[:, :, :], place_c[:, 0], ALU.subtract))
            link(dve.tensor_tensor(place_c[:, 1], place_c[:, 1], per_expert(upto_first[:, :, NTOK - 1]), ALU.add))
            pick(pos[:, :, :], place_c[:, :, :, :])
            link(dve.tensor_scalar(keep[:, :, :], pos[:, :, :], float(CAP), None, ALU.is_lt))
            dve.wait_ge(s_gexp, 2)
            gsteps = [2]

            def glink(ins):
                gsteps[0] += 1
                ins.then_inc(s_gate, 1)
                dve.wait_ge(s_gate, gsteps[0])

            glink(dve.tensor_reduce(gsum[:, :], exps[:, :, :], AX.X, ALU.add))
            glink(dve.reciprocal(gate[0][:, :], gsum[:, :]))
            glink(dve.tensor_tensor(gate[1][:, :], gate[0][:, :], exp2[:, :], ALU.mult))
            glink(dve.scalar_tensor_tensor(denom[:, :], gate[0][:, :], 1e-9, gate[1][:, :], ALU.add, ALU.add))
            glink(dve.reciprocal(gsum[:, :], denom[:, :]))
            for c in range(TOP):
                glink(dve.tensor_tensor(gate[c][:, :], gate[c][:, :], gsum[:, :], ALU.mult))
                glink(dve.tensor_tensor(gate[c][:, :], gate[c][:, :], keep[:, c, :], ALU.mult))

            def dve_step(q, w, has):
                if has(LEAD):
                    from_column(q, w + LEAD)
                if has(2):
                    copy_w1(q, w + 2)
                if has(0):
                    to_column(q, w)
                    copy_results(q, w)

            run_tiles(dve, dve_step)

            for k in range(NG):
                dve.wait_ge(s_yload[k % LANES], 32 * (k // LANES + 1))
                for c, y in enumerate((v[k % LANES], c_in[k % LANES])):
                    if c:
                        dve.wait_ge(s_first, k + 1)
                    for b in range(GB):
                        t = GB * k + b
                        last = dve.scalar_tensor_tensor(x2[:, t, :], y[:, b, 0:D], gate[c][:, t:t + 1], x2[:, t, :],
                                                        ALU.mult, ALU.add)
                    last.then_inc(s_both if c else s_first, 1)

        @block.gpsimd
        def _(pool):
            pool.memset(ident[:, :], 0.0).then_inc(s_ident, 1)
            pool.memset(ones_col[:, :], 1.0)
            pool.memset(neg_half[:, :], -0.5)
            for l in range(LANES):
                pool.memset(v[l][:, :, D:], 1.0)
            pool.wait_ge(s_ident, 1)
            pool.affine_select(out=ident[:, :], in_=ident[:, :], compare_op=ALU.not_equal, fill=1.0, base=0,
                               pattern=[[-1, P]], channel_multiplier=1).then_inc(s_ident, 1)
            pool.memset(b_rows[:, :], 0.0).then_inc(s_bzero, 1)
            pool.memset(ones_bf[:, :], 1.0).then_inc(s_const, 1)
            pool.wait_ge(s_const, 1)
            pool.affine_select(out=before[:, :], in_=ones_bf[:, :], compare_op=ALU.is_gt, fill=0.0, base=0,
                               pattern=[[1, P]], channel_multiplier=-1).then_inc(s_const, 1)
            pool.iota(iota_i[:, :], [[1, P]], base=0, channel_multiplier=0).then_inc(s_iota, 1)
            pool.iota(row_i[:, :], [[1, 1]], base=0, channel_multiplier=1).then_inc(s_iota, 1)
            pool.memset(restart[:, :, :], 1.0).then_inc(s_iota, 1)
            pool.memset(zero_bf[:, :], 0.0).then_inc(s_iotaf, 1)
            pool.wait_ge(s_iota, 3)
            pool.tensor_copy(iota_f[:, :], iota_i[:, :]).then_inc(s_iotaf, 1)
            pool.tensor_copy(iota_b[:, :], iota_i[:, :]).then_inc(s_iotaf, 1)
            pool.tensor_copy(row_f[:, :], row_i[:, :]).then_inc(s_iotaf, 1)
            pool.memset(restart[:, :, 0:1], 0.0).then_inc(s_iotaf, 1)
            def inverse_root(column, ready, done, times):
                pool.wait_ge(ready, times)
                pool.tensor_tensor(column[:, :], column[:, :], neg_half[:, :], ALU.pow).then_inc(done, 1)

            for slot in range(SLOTS):
                now = at_slot(slot)
                if "attend" in now:
                    l, _, n = now["attend"]
                    pool.wait_ge(s_zi, nth(l, n))
                    pool.tensor_tensor(prob[l][:, :, :], prob[l][:, :, :],
                                       zinv[l][:, :].unsqueeze(2).to_broadcast([P, GB, P]), ALU.mult)\
                        .then_inc(s_at, 1)
                if "score" in now:
                    l, _, n = now["score"]
                    inverse_root(rms[l], s_ms, s_rms, nth(l, n))
                if "measure" in now:
                    l, r, _ = now["measure"]
                    inverse_root(rstd[l], s_xve, s_xrs, nth(l, r))
                if "square" in now:
                    l, r, _ = now["square"]
                    inverse_root(crms[l], s_cms, s_crms, nth(l, r))
                if "update" in now:
                    l, _, n = now["update"]
                    pool.wait_ge(s_n, nth(l, n))
                    pool.tensor_tensor(hn[l][:, :, :], hT[l][:, :, :], tr[l][:, :, :], ALU.subtract)\
                        .then_inc(s_hmn, 1)
                if "attend" in now:
                    l, _, n = now["attend"]
                    pool.wait_ge(s_hhi, nth(l, n))
                    pool.tensor_tensor(h_lo[l][:, :, :], hT[l][:, :, :], h_hi[l][:, :, :].bitcast(F32),
                                       ALU.subtract).then_inc(s_hlo, 1)
                    pool.wait_ge(s_uTe, nth(l, n))
                    pool.tensor_tensor(u_lo[l][:, :, :], uT[l][:, :, :], u_hi[l][:, :, :].bitcast(F32),
                                       ALU.subtract).then_inc(s_ulo, 1)

                if "weigh" in now:
                    l, r, _ = now["weigh"]
                    inverse_root(rstd[l], s_fve, s_frs, nth(l, r))
            pool.wait_ge(s_intile, 1)
            for k in range(NP // 8):
                if k >= 2:
                    pool.wait_ge(s_hotrow, k - 1)
                pool.tensor_tensor(row_far[k % 2][:, :, :],
                                   in_tile[:, 8 * k:8 * k + 8].unsqueeze(2).to_broadcast([P, 8, P]),
                                   iota_b[:, :].unsqueeze(1).to_broadcast([P, 8, P]), ALU.subtract)\
                    .then_inc(s_far, 1)

            for l in range(LANES):
                pool.wait_ge(s_lnst[l], 16 * ROUNDS)

            def gather(q, w):
                pool.wait_ge(s_fcol, num(q, w) + 1)
                wait_pos(pool, s_xp, num(q, w) - RB + 1)
                pool.sem_inc(s_go, 1)
                pool.indirect_dma_start(rows[w % RB][:, :], None, ln_dram,
                                        bass.IndirectOffsetOnAxis(ap=from_col[w % RB][:, 0:1], axis=0))\
                    .then_inc(s_rows[w % RB], 16)

            def scatter(q, w):
                pool.wait_ge(s_tcol, num(q, w) + 1)
                pool.wait_ge(s_ye, num(q, w) + 1)
                pool.sem_inc(s_go, 1)
                pool.indirect_dma_start(y_dram, bass.IndirectOffsetOnAxis(ap=to_col[w % RB][:, 0:1], axis=0),
                                        results[w % RB][:, :], None, bounds_check=TOP * T - 1, oob_is_err=False)\
                    .then_inc(s_back[w % RB], 16)

            for j in range(LEAD):
                gather(0, j)

            def pool_step(q, w, has):
                if has(LEAD):
                    gather(q, w + LEAD)
                if has(-1):
                    scatter(q, w - 1)

            run_tiles(pool, pool_step)



def kernel(**inputs):
    import numpy as _np
    import concourse.bacc as _bacc
    from concourse import mybir as _mybir
    from concourse.bass_utils import run_bass_kernel_spmd as _run

    nc = _bacc.Bacc("TRN2", target_bir_lowering=False, num_devices=1)
    arrays, args = {}, []
    w = {k.removeprefix("L0_").removeprefix("xattn_").removeprefix("ffn_"): _np.asarray(a) for k, a in inputs.items()}
    D = w["Wq"].shape[0]

    def turned(m):
        return m.reshape(3, D, D).transpose(2, 0, 1)

    laid_out = {
        "x": w["x"], "ctx": w["ctx_1024"],
        "proj": _np.stack([w["Wk"], w["Wq"], w["Wv"].T], axis=1),
        "gru": _np.stack([turned(w["gru_wih"]), turned(w["gru_whh"])], axis=1),
        "columns": _np.concatenate([w["gru_bih"].reshape(3, D), w["gru_bhh"].reshape(3, D),
                                    w["slot_norm_w"][None], w["input_norm_w"][None]]).T,
        "Wg": w["Wg"], "W1": w["W1"], "b1": w["b1"].reshape(len(w["b1"]), -1, 128).transpose(2, 0, 1), "W2": w["W2"], "b2": w["b2"],
    }
    for name, a in laid_out.items():
        a = _np.ascontiguousarray(a)
        arrays[f"in_{name}"] = a
        args.append(nc.dram_tensor(f"in_{name}", a.shape, _mybir.dt.from_np(a.dtype), kind="ExternalInput").ap())
    out = nc.dram_tensor("out_0", tuple(inputs["x"].shape), F32, kind="ExternalOutput").ap()
    xattn_moe_kernel(nc, *args, out)
    r = _run(nc, [arrays], core_ids=[0])
    return r.results[0]["out_0"]
```
